# Optimizing a Trainium2 kernel written in Bass

```python
import numpy as np
import jax
import jax.numpy as jnp

def _softmax(x, axis=-1):
    return jax.nn.softmax(x, axis=axis)
def _gelu(x):
    return jax.nn.gelu(x, approximate=True)
def _silu(x):
    return jax.nn.silu(x)
def _sigmoid(x):
    return jax.nn.sigmoid(x)
def _layernorm(x, axis=-1, eps=1e-5):
    m = jnp.mean(x, axis=axis, keepdims=True)
    v = jnp.var(x, axis=axis, keepdims=True)
    return (x - m) / jnp.sqrt(v + eps)
def _scatter_add(tgt, idx, src, axis=0):
    return tgt.at[idx].add(src)
def _segment_sum(src, seg, n):
    return jax.ops.segment_sum(src, seg, n)

kernel_name = 'mk_conv_preact_d2_conv_nchw384_80dfd4'

def setup_inputs(seed: int = 0):
    np.random.seed(seed)
    _w = jnp.asarray
    def _rec_inputs():
        import jax
        import jax.numpy as jnp
        _gk = jax.random.key(seed)
        x = -0.0003483 + 1 * jax.random.normal(jax.random.fold_in(_gk, 1), (1, 384, 192, 192), jnp.float32)
        return x
    x = _rec_inputs()
    def _L0_conv_setup():
        import jax, jax.numpy as jnp
        import numpy as np
        from jax import lax
        DIM = 384
        HEADS = 8
        DS = 2

        def _topk_softmax(attn, kk):
            idx = lax.top_k(attn, kk)[1]
            mask = jax.nn.one_hot(idx, attn.shape[-1], dtype=attn.dtype).sum(-2)
            return jax.nn.softmax(jnp.where(mask > 0, attn, -jnp.inf), axis=-1)
        key = jax.random.key(seed)
        ks = jax.random.split(key, 6)
        d = DIM
        x = jax.random.normal(ks[0], (1, d, 192, 192), jnp.float32)
        w_qkv = jax.random.normal(ks[1], (3 * d, d), jnp.float32) * 0.02
        b_qkv = jnp.zeros((3 * d,), jnp.float32)
        w_dw = jax.random.normal(ks[2], (3 * d, 1, 3, 3), jnp.float32) * 0.1
        b_dw = jnp.zeros((3 * d,), jnp.float32)
        w_proj = jax.random.normal(ks[3], (d, d), jnp.float32) * 0.02
        b_proj = jnp.zeros((d,), jnp.float32)
        temperature = jnp.ones((HEADS, 1, 1), jnp.float32)
        a1 = jnp.array([0.2], jnp.float32)
        a2 = jnp.array([0.2], jnp.float32)
        a3 = jnp.array([0.2], jnp.float32)
        a4 = jnp.array([0.2], jnp.float32)
        return {'x': x, 'w_qkv': w_qkv, 'b_qkv': b_qkv, 'w_dw': w_dw, 'b_dw': b_dw, 'w_proj': w_proj, 'b_proj': b_proj, 'temperature': temperature, 'a1': a1, 'a2': a2, 'a3': a3, 'a4': a4}
    _L0_conv_all = _L0_conv_setup()
    _L0_conv_in = {k: v for k, v in _L0_conv_all.items() if k in ('w_qkv', 'b_qkv', 'w_dw', 'b_dw', 'w_proj', 'b_proj', 'temperature', 'a1', 'a2', 'a3', 'a4', )}
    del _L0_conv_all

    def _L1_conv_setup():
        import jax, jax.numpy as jnp
        import numpy as np
        EPS = 1e-05

        def _dwconv(x, w, pad):
            return jax.lax.conv_general_dilated(x, w, window_strides=(1, 1), padding=[(pad, pad), (pad, pad)], feature_group_count=w.shape[0], dimension_numbers=('NCHW', 'OIHW', 'NCHW'))

        def _bn(y, g, b, m, v):
            scale = (g / jnp.sqrt(v + EPS))[None, :, None, None]
            shift = (b - m * g / jnp.sqrt(v + EPS))[None, :, None, None]
            return y * scale + shift
        key = jax.random.key(seed)
        ks = jax.random.split(key, 16)
        C, KL, KS = (384, 13, 3)
        N, H, W = (16, 64, 64)
        inp = {'x': jax.random.normal(ks[0], (N, C, H, W), jnp.float32), 'w_large': jax.random.normal(ks[1], (C, 1, KL, KL), jnp.float32) * 0.05, 'w_small': jax.random.normal(ks[2], (C, 1, KS, KS), jnp.float32) * 0.2, 'g_l': jax.random.normal(ks[3], (C,), jnp.float32), 'b_l': jax.random.normal(ks[4], (C,), jnp.float32), 'm_l': jax.random.normal(ks[5], (C,), jnp.float32), 'v_l': jax.random.uniform(ks[6], (C,), jnp.float32, 0.5, 1.5), 'g_s': jax.random.normal(ks[7], (C,), jnp.float32), 'b_s': jax.random.normal(ks[8], (C,), jnp.float32), 'm_s': jax.random.normal(ks[9], (C,), jnp.float32), 'v_s': jax.random.uniform(ks[10], (C,), jnp.float32, 0.5, 1.5), 'g_i': jax.random.normal(ks[11], (C,), jnp.float32), 'b_i': jax.random.normal(ks[12], (C,), jnp.float32), 'm_i': jax.random.normal(ks[13], (C,), jnp.float32), 'v_i': jax.random.uniform(ks[14], (C,), jnp.float32, 0.5, 1.5)}
        return inp
    _L1_conv_all = _L1_conv_setup()
    _L1_conv_in = {k: v for k, v in _L1_conv_all.items() if k in ('w_large', 'w_small', 'g_l', 'b_l', 'm_l', 'v_l', 'g_s', 'b_s', 'm_s', 'v_s', 'g_i', 'b_i', 'm_i', 'v_i', )}
    del _L1_conv_all

    return {
        "x": x,
        "L0_conv_w_qkv": _L0_conv_in["w_qkv"],
        "L0_conv_b_qkv": _L0_conv_in["b_qkv"],
        "L0_conv_w_dw": _L0_conv_in["w_dw"],
        "L0_conv_b_dw": _L0_conv_in["b_dw"],
        "L0_conv_w_proj": _L0_conv_in["w_proj"],
        "L0_conv_b_proj": _L0_conv_in["b_proj"],
        "L0_conv_temperature": _L0_conv_in["temperature"],
        "L0_conv_a1": _L0_conv_in["a1"],
        "L0_conv_a2": _L0_conv_in["a2"],
        "L0_conv_a3": _L0_conv_in["a3"],
        "L0_conv_a4": _L0_conv_in["a4"],
        "L1_conv_w_large": _L1_conv_in["w_large"],
        "L1_conv_w_small": _L1_conv_in["w_small"],
        "L1_conv_g_l": _L1_conv_in["g_l"],
        "L1_conv_b_l": _L1_conv_in["b_l"],
        "L1_conv_m_l": _L1_conv_in["m_l"],
        "L1_conv_v_l": _L1_conv_in["v_l"],
        "L1_conv_g_s": _L1_conv_in["g_s"],
        "L1_conv_b_s": _L1_conv_in["b_s"],
        "L1_conv_m_s": _L1_conv_in["m_s"],
        "L1_conv_v_s": _L1_conv_in["v_s"],
        "L1_conv_g_i": _L1_conv_in["g_i"],
        "L1_conv_b_i": _L1_conv_in["b_i"],
        "L1_conv_m_i": _L1_conv_in["m_i"],
        "L1_conv_v_i": _L1_conv_in["v_i"],
    }

def reference(x, L0_conv_w_qkv, L0_conv_b_qkv, L0_conv_w_dw, L0_conv_b_dw, L0_conv_w_proj, L0_conv_b_proj, L0_conv_temperature, L0_conv_a1, L0_conv_a2, L0_conv_a3, L0_conv_a4, L1_conv_w_large, L1_conv_w_small, L1_conv_g_l, L1_conv_b_l, L1_conv_m_l, L1_conv_v_l, L1_conv_g_s, L1_conv_b_s, L1_conv_m_s, L1_conv_v_s, L1_conv_g_i, L1_conv_b_i, L1_conv_m_i, L1_conv_v_i):
    import jax
    import jax.numpy as jnp
    def _L0_conv_ref(x, w_qkv, b_qkv, w_dw, b_dw, w_proj, b_proj, temperature, a1, a2, a3, a4):
        import jax, jax.numpy as jnp
        import numpy as np
        from jax import lax
        DIM = 384
        HEADS = 8
        DS = 2

        def _topk_softmax(attn, kk):
            idx = lax.top_k(attn, kk)[1]
            mask = jax.nn.one_hot(idx, attn.shape[-1], dtype=attn.dtype).sum(-2)
            return jax.nn.softmax(jnp.where(mask > 0, attn, -jnp.inf), axis=-1)
        b, c, h, w = x.shape
        qkv = jnp.einsum('bchw,oc->bohw', x, w_qkv) + b_qkv[None, :, None, None]
        hs, ws = (h // DS, w // DS)
        qkv = qkv.reshape(b, 3 * c, hs, DS, ws, DS).max(axis=(3, 5))
        qkv = lax.conv_general_dilated(qkv, w_dw, (1, 1), 'SAME', feature_group_count=3 * c, dimension_numbers=('NCHW', 'OIHW', 'NCHW'))
        qkv = qkv + b_dw[None, :, None, None]
        q, k, v = jnp.split(qkv, 3, axis=1)
        hw = hs * ws
        C = c // HEADS
        q = q.reshape(b, HEADS, C, hw)
        k = k.reshape(b, HEADS, C, hw)
        v = v.reshape(b, HEADS, C, hw)
        q = q / jnp.clip(jnp.linalg.norm(q, axis=-1, keepdims=True), 1e-12)
        k = k / jnp.clip(jnp.linalg.norm(k, axis=-1, keepdims=True), 1e-12)
        attn = jnp.einsum('bhcn,bhdn->bhcd', q, k) * temperature[None]
        out = _topk_softmax(attn, C // 2) @ v * a1 + _topk_softmax(attn, C * 2 // 3) @ v * a2 + _topk_softmax(attn, C * 3 // 4) @ v * a3 + _topk_softmax(attn, C * 4 // 5) @ v * a4
        out = out.reshape(b, c, hs, ws)
        out = jax.nn.gelu(out, approximate=False)
        out = jnp.repeat(jnp.repeat(out, DS, axis=2), DS, axis=3)
        out = jnp.einsum('bchw,oc->bohw', out, w_proj) + b_proj[None, :, None, None]
        return out

    def _L1_conv_ref(x, w_large, w_small, g_l, b_l, m_l, v_l, g_s, b_s, m_s, v_s, g_i, b_i, m_i, v_i):
        import jax, jax.numpy as jnp
        import numpy as np
        EPS = 1e-05

        def _dwconv(x, w, pad):
            return jax.lax.conv_general_dilated(x, w, window_strides=(1, 1), padding=[(pad, pad), (pad, pad)], feature_group_count=w.shape[0], dimension_numbers=('NCHW', 'OIHW', 'NCHW'))

        def _bn(y, g, b, m, v):
            scale = (g / jnp.sqrt(v + EPS))[None, :, None, None]
            shift = (b - m * g / jnp.sqrt(v + EPS))[None, :, None, None]
            return y * scale + shift
        kl = w_large.shape[-1]
        ks = w_small.shape[-1]
        out = _bn(_dwconv(x, w_large, kl // 2), g_l, b_l, m_l, v_l) + _bn(_dwconv(x, w_small, ks // 2), g_s, b_s, m_s, v_s) + _bn(x, g_i, b_i, m_i, v_i)
        return out

    def _gn(v, G=32, eps=1e-5):
        B_, C_, H_, W_ = v.shape
        g = v.reshape(B_, G, C_ // G, H_, W_)
        m = jnp.mean(g, axis=(2, 3, 4), keepdims=True)
        s = jnp.var(g, axis=(2, 3, 4), keepdims=True)
        return ((g - m) / jnp.sqrt(s + eps)).reshape(v.shape)

    def _ln_c(v, eps=1e-6):
        m = jnp.mean(v, axis=1, keepdims=True)
        s = jnp.var(v, axis=1, keepdims=True)
        return (v - m) / jnp.sqrt(s + eps)

    def _ln_t(v, eps=1e-5):
        m = jnp.mean(v, axis=-1, keepdims=True)
        s = jnp.var(v, axis=-1, keepdims=True)
        return (v - m) / jnp.sqrt(s + eps)

    def _to_tokens(v):
        B_, C_, H_, W_ = v.shape
        return v.reshape(B_, C_, H_ * W_).transpose(0, 2, 1)
    def _from_tokens(t, like):
        B_, C_, H_, W_ = like.shape
        return t.transpose(0, 2, 1).reshape(B_, C_, H_, W_)

    x = x + _L0_conv_ref(_gn(x), L0_conv_w_qkv, L0_conv_b_qkv, L0_conv_w_dw, L0_conv_b_dw, L0_conv_w_proj, L0_conv_b_proj, L0_conv_temperature, L0_conv_a1, L0_conv_a2, L0_conv_a3, L0_conv_a4)
    x = x + _L1_conv_ref(_gn(x), L1_conv_w_large, L1_conv_w_small, L1_conv_g_l, L1_conv_b_l, L1_conv_m_l, L1_conv_v_l, L1_conv_g_s, L1_conv_b_s, L1_conv_m_s, L1_conv_v_s, L1_conv_g_i, L1_conv_b_i, L1_conv_m_i, L1_conv_v_i)
    return x


_drawn_inputs = setup_inputs


def setup_inputs(seed=0):
    import zlib

    import numpy as np

    out = dict(_drawn_inputs(seed))
    spreads = {'L0_conv_b_qkv': (0.0, 0.8),
     'L0_conv_b_dw': (0.0, 0.8),
     'L0_conv_b_proj': (0.0, 0.339),
     'L0_conv_temperature': (1.0, 0.6)}
    factors = {'L0_conv_w_qkv': 8.0, 'L0_conv_w_dw': 8.0, 'L0_conv_w_proj': 8.0}
    for name, (base, spread) in spreads.items():
        noise = np.random.default_rng([zlib.crc32(name.encode()), seed]).standard_normal(out[name].shape)
        drawn = base * np.exp(spread * noise) if base else spread * noise
        out[name] = jnp.asarray(drawn.astype(out[name].dtype))
    for name, factor in factors.items():
        out[name] = (out[name] * factor).astype(out[name].dtype)
    return out
```

```python
from contextlib import ExitStack

import concourse.bass as bass
from concourse import mybir

ALU = mybir.AluOpType
ACT = mybir.ActivationFunctionType
AX = mybir.AxisListType
F32 = mybir.dt.float32
F16 = mybir.dt.float16

P = 128
C = 384
CB = C // P
H = W = 192
GROUPS = 32
GC = C // GROUPS
ROWS = 8
STEPS = H // ROWS
CHUNK = ROWS * W
QO = 3 * C // P
PR = ROWS // 2
PW = W // 2
PX = PR * PW
VROWS = H // 2 + PR
HEADS = 8
HC = C // HEADS
PAIR = 2 * HC
NPAIR = C // PAIR
TOPK = (HC // 2, HC * 2 // 3, HC * 3 // 4, HC * 4 // 5)
TAKEN = -3.0e38
SCALE = 64.0
UNSCALE = 1.0 / (SCALE * SCALE)

KL = 13
PAD = KL // 2
KS = 3
TH, TW = 8, 16
TI = H // TH + 1
TJ = W // TW + 1
OI, OJ = H // TH, W // TW
NS, NU = 3, 2
XW = TJ * TW
GRP = 16
NG = C // GRP
JR = NS * TH + TH - 1
JX = NU * TW + TW - 1
TCH = TI * GRP * TJ
BAND = P // GRP
NBAND = OI // BAND
KRUN = NS * TH * TW * NU * 2


def at(step, n):
    return isinstance(step, int) and step == n


def address(eng, elements, size=4):
    if not isinstance(elements, int):
        eng.compute_val(elements * size)
    return elements


def group_affine(nc, tag, stats, nstat, chan_dram, group_dram, mean, rstd):
    with ExitStack() as ctx:
        def sb(name, shape):
            return ctx.enter_context(nc.sbuf_tensor(f"{tag}_{name}", shape, F32))

        def sem(name):
            return ctx.enter_context(nc.semaphore(f"{tag}_{name}"))

        chan = sb("chan", [P, CB, 2])
        grp = sb("grp", [GROUPS, GC, 2])
        dev = sb("dev", [GROUPS, GC])
        gm = sb("gm", [GROUPS, 4])
        gout = sb("gout", [GROUPS, GC, 2])
        back = sb("back", [P, CB, 2])
        eps = sb("eps", [P, 1])
        link, std_ready, moved = sem("link"), sem("std_ready"), sem("moved")
        agg_ready, gout_ready = sem("agg_ready"), sem("gout_ready")
        block = ctx.enter_context(nc.Block())

        @block.sync
        def _(sp):
            sp.wait_ge(agg_ready, CB)
            sp.dma_start(chan_dram.rearrange("(b p) s -> p b s", p=P), chan[:, :, :],
                         allow_slow_non_contiguous=True).then_inc(moved, 16)
            sp.wait_ge(moved, 16)
            sp.dma_start(grp[:, :, :], chan_dram.rearrange("(g k) s -> g k s", k=GC)).then_inc(moved, 16)
            sp.wait_ge(gout_ready, 1)
            sp.dma_start(group_dram.rearrange("(g k) s -> g k s", k=GC), gout[:, :, :]).then_inc(moved, 16)
            sp.wait_ge(moved, 48)
            sp.dma_start(back[:, :, :], group_dram.rearrange("(b p) s -> p b s", p=P),
                         allow_slow_non_contiguous=True).then_inc(moved, 16)

        @block.scalar
        def _(act):
            act.wait_ge(link, 8)
            nc.scalar.activation(gm[:, 3:4], gm[:, 2:3], ACT.Sqrt, bias=eps[0:GROUPS, :]).then_inc(std_ready, 1)

        @block.vector
        def _(dve):
            count = [0]

            def chained(ins):
                count[0] += 1
                ins.then_inc(link, 1)
                dve.wait_ge(link, count[0])

            chained(nc.vector.memset(eps[:, :], 1e-5))
            for b in range(CB):
                nc.vector.bn_aggr(chan[:, b, :], stats[:, b, :, :].rearrange("p n s -> p (n s)")).then_inc(agg_ready, 1)
            dve.wait_ge(moved, 32)
            chained(nc.vector.tensor_reduce(gm[:, 0:1], grp[:, :, 0], AX.X, ALU.add))
            chained(nc.vector.tensor_scalar(gm[:, 0:1], gm[:, 0:1], 1.0 / GC, None, ALU.mult))
            chained(nc.vector.tensor_scalar(dev[:, :], grp[:, :, 0], gm[:, 0:1], None, ALU.subtract))
            chained(nc.vector.tensor_tensor(dev[:, :], dev[:, :], dev[:, :], ALU.mult))
            chained(nc.vector.tensor_tensor(dev[:, :], dev[:, :], grp[:, :, 1], ALU.add))
            chained(nc.vector.tensor_reduce(gm[:, 1:2], dev[:, :], AX.X, ALU.add))
            nc.vector.tensor_scalar(gm[:, 2:3], gm[:, 1:2], 1.0 / GC, None, ALU.mult).then_inc(link, 1)
            count[0] += 1
            dve.wait_ge(std_ready, 1)
            chained(nc.vector.reciprocal(gm[:, 1:2], gm[:, 3:4]))
            chained(nc.vector.tensor_copy(gout[:, :, 0], gm[:, 0:1].to_broadcast([GROUPS, GC])))
            nc.vector.tensor_copy(gout[:, :, 1], gm[:, 1:2].to_broadcast([GROUPS, GC])).then_inc(gout_ready, 1)
            dve.wait_ge(moved, 64)
            nc.vector.tensor_copy(mean[:, :], back[:, :, 0])
            nc.vector.tensor_copy(rstd[:, :], back[:, :, 1]).then_inc(link, 1)
            count[0] += 1
            dve.wait_ge(link, count[0])


def stage_statistics(nc, x3, stats):
    XBUFS = 4
    REC = CHUNK // 512
    with ExitStack() as ctx:
        xs = ctx.enter_context(nc.sbuf_tensor("st_x", [P, XBUFS, CB, CHUNK], F32))
        x_in = [ctx.enter_context(nc.semaphore(f"st_x_in{i}")) for i in range(XBUFS)]
        x_used = ctx.enter_context(nc.semaphore("st_x_used"))
        block = ctx.enter_context(nc.Block())
        src = x3.rearrange("(b p) n -> p b n", p=P)

        @block.sync
        def _(sp):
            for i in range(XBUFS):
                sp.dma_start(xs[:, i], src[:, :, i * CHUNK:(i + 1) * CHUNK]).then_inc(x_in[i], 16)
            with sp.Fori(1, STEPS // XBUFS) as r:
                for i in range(XBUFS):
                    address(sp, (r * XBUFS + i) * CHUNK)
                    sp.wait_ge(x_used, r * XBUFS + i - XBUFS + 1)
                    sp.dma_start(xs[:, i], src[:, :, bass.ds((r * XBUFS + i) * CHUNK, CHUNK)]).then_inc(x_in[i], 16)

        @block.vector
        def _(dve):
            with dve.Fori(0, STEPS // XBUFS) as r:
                for i in range(XBUFS):
                    dve.wait_ge(x_in[i], r * 16 + 16)
                    for b in range(CB):
                        for k in range(REC):
                            ins = nc.vector.bn_stats(
                                stats[:, b, bass.ds((r * XBUFS + i) * REC + k, 1), :].rearrange("p a s -> p (a s)"),
                                xs[:, i, b, k * 512:(k + 1) * 512])
                    ins.then_inc(x_used, 1)


def stage_qkv(nc, x3, wT, b_qkv, w_dw, b_dw, mean, rstd, ident, rq_dram, v_dram, gram):
    UNITS = STEPS + 1
    NQB = 4
    NTB = 3
    PASSES = 3
    GPS = PR * QO
    QK = 2 * CB
    NTP = PX // P
    NT = 2 * NTP
    TAPS = KS * KS
    with ExitStack() as ctx:
        def sb(name, shape, dt=F32):
            return ctx.enter_context(nc.sbuf_tensor(f"qk_{name}", shape, dt))

        def ps(name, shape):
            return ctx.enter_context(nc.psum_tensor(f"qk_{name}", shape, F32))

        def sem(name):
            return ctx.enter_context(nc.semaphore(f"qk_{name}"))

        xf = sb("xf", [P, 2, CB, CHUNK])
        xhi = sb("xhi", [P, 2, CB, CHUNK], F16)
        xlo = sb("xlo", [P, 2, CB, CHUNK], F16)
        whi = sb("whi", [P, CB, 3 * C], F16)
        wlo = sb("wlo", [P, CB, 3 * C], F16)
        pool = sb("pool", [P, 2, QO, PR + 2, PW + 2])
        dw = sb("dw", [P, 2, QO, PX])
        pixT = sb("pixT", [P, NTP, 2, C])
        sq = sb("sq", [P, PX])
        bq = sb("bq", [P, QO])
        bd = sb("bd", [P, QO])
        wd = sb("wd", [P, QO, TAPS])
        sx = sb("sx", [P, CB])
        bx = sb("bx", [P, CB])
        nrm = sb("nrm", [P, QK, UNITS])
        tot = sb("tot", [P, 3, QK])
        wst = xf[:, :, :, :].rearrange("p a b n -> p (a b n)")[:, 0:CB * 3 * C].rearrange("p (b n) -> p b n", b=CB)
        qbank = [ps(f"qb{i}", [P, 512]) for i in range(NQB)]
        tbank = [ps(f"tb{i}", [P, 512]) for i in range(NTB)]

        w_in, c_in = sem("w_in"), sem("c_in")
        x_in = [sem("x_in0"), sem("x_in1")]
        prep, whi_ready, w_ready, zeroed = sem("prep"), sem("whi_ready"), sem("w_ready"), sem("zeroed")
        norm_ready, hi_ready, lo_ready = sem("norm_ready"), sem("hi_ready"), sem("lo_ready")
        qkv_done, max_done = sem("qkv_done"), sem("max_done")
        bias_done, halo_done, tap0_done = sem("bias_done"), sem("halo_done"), sem("tap0_done")
        taps_done, dw_done, below_zero = sem("taps_done"), sem("dw_done"), sem("below_zero")
        tr_done, tr_out, gram_done, sq_done = sem("tr_done"), sem("tr_out"), sem("gram_done"), sem("sq_done")
        v_out = [sem("v_out0"), sem("v_out1")]
        fin, root_done, rn_out = sem("fin"), sem("root_done"), sem("rn_out")
        block = ctx.enter_context(nc.Block())
        src = x3.rearrange("(b p) n -> p b n", p=P)
        vdst = v_dram.rearrange("(b p) n -> p b n", p=P)

        LAST = UNITS + 1

        PEEL = 4

        def run(eng, step, tail=STEPS):
            for t in range(PEEL):
                step(t, t % 2)
            with eng.Fori(PEEL // 2, tail // 2) as i:
                step(i * 2, 0, True)
                step(i * 2 + 1, 1, True)
            for t in range(tail, LAST + 1):
                step(t, t % 2)

        @block.sync
        def _(sp):
            sp.dma_start(wst, wT.rearrange("(b p) n -> p b n", p=P)).then_inc(w_in, 16)
            sp.dma_start(bq[:, :], b_qkv.rearrange("(b p) -> p b", p=P), allow_slow_non_contiguous=True).then_inc(c_in, 16)
            sp.dma_start(bd[:, :], b_dw.rearrange("(b p) -> p b", p=P), allow_slow_non_contiguous=True).then_inc(c_in, 16)
            sp.dma_start(wd[:, :, :], w_dw.rearrange("(b p) o y x -> p b (o y x)", p=P)).then_inc(c_in, 16)
            sp.wait_ge(w_ready, 1)
            for t in range(2):
                sp.dma_start(xf[:, t], src[:, :, t * CHUNK:(t + 1) * CHUNK]).then_inc(x_in[t], 16)

            def step(t, par, inner=False):
                if inner or t + 2 < STEPS:
                    address(sp, (t + 2) * CHUNK)
                    sp.wait_ge(lo_ready, t + 1)
                    sp.dma_start(xf[:, par], src[:, :, bass.ds((t + 2) * CHUNK, CHUNK)]).then_inc(x_in[par], 16)
                if inner or 0 <= t - 1 < UNITS:
                    address(sp, (t - 1) * PX)
                    sp.wait_ge(dw_done, t)
                    sp.dma_start(vdst[:, :, bass.ds((t - 1) * PX, PX)], dw[:, 1 - par, QK:QO, :]).then_inc(v_out[1 - par], 16)

            run(sp, step, STEPS - 2)
            sp.wait_ge(fin, 4)
            sp.dma_start(rq_dram.rearrange("(b p) -> p b", p=P), tot[:, 2, :],
                         allow_slow_non_contiguous=True).then_inc(rn_out, 16)
            sp.wait_ge(rn_out, 16)
            sp.wait_ge(v_out[0], 16 * (UNITS // 2 + 1))
            sp.wait_ge(v_out[1], 16 * (UNITS // 2))

        @block.scalar
        def _(act):
            act.wait_ge(w_in, 16)
            nc.scalar.activation(whi[:, :, :], wst, ACT.Copy, scale=SCALE).then_inc(whi_ready, 1)
            act.wait_ge(prep, 2)
            act.wait_ge(c_in, 48)

            def split(t, par, first=False):
                act.wait_ge(x_in[par], (t // 2) * 16 + 16 if isinstance(t, int) else (t - par) * 8 + 16)
                for b in range(CB):
                    nc.scalar.activation(xf[:, par, b], xf[:, par, b], ACT.Identity,
                                         bias=bx[:, b:b + 1], scale=sx[:, b:b + 1]).then_inc(norm_ready, 1)
                act.wait_ge(norm_ready, t * CB + CB)
                if not first:
                    act.wait_ge(qkv_done, t * GPS - GPS)
                nc.scalar.activation(xhi[:, par], xf[:, par], ACT.Copy).then_inc(hi_ready, 1)

            split(0, 0, True)

            def step(t, par, inner=False):
                u, up = t - 1, 1 - par
                if inner or 0 <= u < UNITS:
                    real = inner or u < STEPS
                    if real:
                        act.wait_ge(max_done, u * GPS + GPS)
                        if inner or u >= 1:
                            act.wait_ge(dw_done, u)
                    else:
                        act.wait_ge(below_zero, 1)
                    act.wait_ge(zeroed, 2)
                    if inner or u >= 2:
                        act.wait_ge(v_out[up], (u - up) * 8)
                        act.wait_ge(tr_done, u * NT - NT)
                        act.wait_ge(sq_done, u * QK - QK)
                    if real:
                        for o in range(QO):
                            nc.scalar.activation(pool[:, par, o, 0:2, 1:1 + PW], pool[:, up, o, PR:PR + 2, 1:1 + PW],
                                                 ACT.Identity, bias=bq[:, o:o + 1], scale=UNSCALE).then_inc(halo_done, 1)
                        for o in range(QO):
                            act.wait_ge(halo_done, u * QO + o + 1)
                            nc.scalar.activation(pool[:, up, o, 2:2 + PR, 1:1 + PW], pool[:, up, o, 2:2 + PR, 1:1 + PW],
                                                 ACT.Identity, bias=bq[:, o:o + 1], scale=UNSCALE).then_inc(bias_done, 1)
                    for o in range(QO):
                        if real:
                            act.wait_ge(bias_done, u * QO + o + 1)
                        nc.scalar.activation(dw[:, up, o, :].rearrange("p (y x) -> p y x", y=PR), pool[:, up, o, 0:PR, 0:PW],
                                             ACT.Identity, bias=bd[:, o:o + 1], scale=wd[:, o, 0:1]).then_inc(tap0_done, 1)
                u = t - 2
                if inner or 0 <= u < UNITS:
                    if inner or u >= 1:
                        act.wait_ge(gram_done, u)
                    for n in range(NT):
                        act.wait_ge(tr_done, u * NT + n + 1)
                        nc.scalar.activation(pixT[:, n // 2, n % 2, :], tbank[n % NTB][:, 0:C], ACT.Copy).then_inc(tr_out, 1)
                    act.wait_ge(dw_done, u + 1)
                    for o in range(QK):
                        if inner or u >= 1 or o >= 1:
                            act.wait_ge(sq_done, u * QK + o)
                        nc.scalar.activation(sq[:, :], dw[:, par, o, :], ACT.Square,
                                             accum_out=nrm[:, o, bass.ds(u, 1)]).then_inc(sq_done, 1)
                if at(t, 0):
                    split(1, 1, True)
                elif inner or t + 1 < STEPS:
                    split(t + 1, 1 - par)

            run(act, step, STEPS - 2)
            act.wait_ge(fin, 1)
            nc.scalar.activation(tot[:, 1, :], tot[:, 0, :], ACT.Sqrt).then_inc(root_done, 1)

        @block.gpsimd
        def _(gp):
            def low(t, par, first=False):
                gp.wait_ge(hi_ready, t + 1)
                if not first:
                    gp.wait_ge(qkv_done, t * GPS - GPS)
                nc.gpsimd.tensor_tensor(xlo[:, par], xf[:, par], xhi[:, par], ALU.subtract).then_inc(lo_ready, 1)

            low(0, 0, True)
            low(1, 1, True)
            with gp.Fori(1, STEPS // 2) as i:
                low(i * 2, 0)
                low(i * 2 + 1, 1)

        @block.vector
        def _(dve):
            nc.vector.tensor_scalar(sx[:, :], rstd[:, :], SCALE, None, ALU.mult).then_inc(prep, 1)
            dve.wait_ge(prep, 1)
            nc.vector.scalar_tensor_tensor(bx[:, :], mean[:, :], -1.0, sx[:, :], ALU.mult, ALU.mult).then_inc(prep, 1)
            nc.vector.memset(pool[:, 0], 0.0).then_inc(zeroed, 1)
            nc.vector.memset(pool[:, 1], 0.0).then_inc(zeroed, 1)
            dve.wait_ge(zeroed, 2)
            dve.wait_ge(whi_ready, 1)
            nc.vector.scalar_tensor_tensor(wlo[:, :, :].rearrange("p b n -> p (b n)"), wst.rearrange("p b n -> p (b n)"),
                                           SCALE, whi[:, :, :].rearrange("p b n -> p (b n)"),
                                           ALU.mult, ALU.subtract).then_inc(w_ready, 1)
            taps = [(o0 + o, k) for o0 in range(0, QO, 3) for k in range(1, TAPS) for o in range(3)]
            LEAD = 6

            def step(t, par, inner=False):
                u, up = t - 1, 1 - par
                convolve = inner or 0 <= u < UNITS
                done = 0
                for g in range(GPS):
                    if inner or t < STEPS:
                        dve.wait_ge(qkv_done, t * GPS + g + 1)
                        if g == 0 and (inner or t >= 2):
                            dve.wait_ge(halo_done, (t - 1) * QO)
                        j, o = g // QO, g % QO
                        nc.vector.tensor_reduce(
                            pool[:, par, o, 2 + j, 1:1 + PW],
                            qbank[g % NQB][:, 0:2 * W].rearrange("p (r x c) -> p x r c", r=2, c=2),
                            AX.XY, ALU.max).then_inc(max_done, 1)
                    if convolve:
                        upto = max(0, (g + 1 - LEAD)) * len(taps) // (GPS - LEAD)
                        for n in range(done, upto):
                            o, k = taps[n]
                            if k == 1:
                                dve.wait_ge(tap0_done, u * QO + o + 1)
                            else:
                                dve.wait_ge(taps_done, u * len(taps) + n - 2)
                            y, x = k // KS, k % KS
                            acc = dw[:, up, o, :].rearrange("p (y x) -> p y x", y=PR)
                            nc.vector.scalar_tensor_tensor(acc, pool[:, up, o, y:y + PR, x:x + PW], wd[:, o, k:k + 1], acc,
                                                           ALU.mult, ALU.add).then_inc(taps_done, 1)
                        done = upto
                if convolve:
                    dve.wait_ge(taps_done, u * len(taps) + len(taps))
                    if at(t, 1):
                        nc.vector.memset(dw[:, up, 0:QK, 0:PW], 0.0).then_inc(dw_done, 1)
                    elif at(t, UNITS):
                        nc.vector.memset(dw[:, up, 0:QK, PW:PX], 0.0).then_inc(dw_done, 1)
                    else:
                        dve.sem_inc(dw_done, 1)
                if at(t, STEPS - 1):
                    nc.vector.memset(pool[:, 0, :, 2:2 + PR, 1:1 + PW], 0.0).then_inc(below_zero, 1)

            run(dve, step, STEPS - 2)
            dve.wait_ge(sq_done, UNITS * QK)
            nc.vector.tensor_reduce(tot[:, 0, :], nrm[:, :, :], AX.X, ALU.add).then_inc(fin, 1)
            dve.wait_ge(root_done, 1)
            nc.vector.tensor_scalar(tot[:, 1, :], tot[:, 1, :], 1e-12, None, ALU.max).then_inc(fin, 1)
            dve.wait_ge(fin, 2)
            nc.vector.reciprocal(tot[:, 2, :], tot[:, 1, :]).then_inc(fin, 2)

        @block.tensor
        def _(pe):
            pe.wait_ge(w_ready, 1)
            TR_AT = {10: range(0, 3), 12: range(3, 6)}
            GRAM_AT = 16

            def transposes(u, par, ns, inner):
                if ns[0] == 0:
                    pe.wait_ge(dw_done, u + 1)
                for n in ns:
                    if inner or u >= 1 or n >= NTB:
                        pe.wait_ge(tr_out, u * NT + n - NTB + 1)
                    px, qk = n // 2, n % 2
                    for b in range(CB):
                        ins = nc.tensor.transpose(tbank[n % NTB][:, b * P:(b + 1) * P],
                                                  dw[:, par, qk * CB + b, px * P:(px + 1) * P], ident[:, :])
                    ins.then_inc(tr_done, 1)

            def grams(u):
                pe.wait_ge(tr_out, u * NT + NT)
                for px in range(NTP):
                    for h in range(NPAIR):
                        first = at(u, 0) and px == 0 and h == 0
                        last = at(u, UNITS - 1) and px == NTP - 1
                        ins = nc.tensor.matmul(gram[0:PAIR, h * PAIR:(h + 1) * PAIR],
                                               pixT[:, px, 0, h * PAIR:(h + 1) * PAIR],
                                               pixT[:, px, 1, h * PAIR:(h + 1) * PAIR],
                                               start=first, stop=last, skip_group_check=True)
                ins.then_inc(gram_done, 1)

            def step(t, par, inner=False):
                tail = inner or 0 <= t - 2 < UNITS
                if inner or t < STEPS:
                    pe.wait_ge(lo_ready, t + 1)
                for g in range(GPS):
                    if inner or t < STEPS:
                        if inner or t >= 1 or g >= NQB:
                            pe.wait_ge(max_done, t * GPS + g - NQB + 1)
                        j, o = g // QO, g % QO
                        n = 0
                        for b in range(CB):
                            for w, x in ((whi, xhi), (whi, xlo), (wlo, xhi)):
                                ins = nc.tensor.matmul(qbank[g % NQB][:, 0:2 * W], w[:, b, o * P:(o + 1) * P],
                                                       x[:, par, b, j * 2 * W:(j + 1) * 2 * W],
                                                       start=n == 0, stop=n == CB * PASSES - 1)
                                n += 1
                        ins.then_inc(qkv_done, 1)
                    if tail and g in TR_AT:
                        transposes(t - 2, par, TR_AT[g], inner)
                    if tail and g == GRAM_AT:
                        grams(t - 2)

            run(pe, step)


def stage_attention(nc, gram, rq_dram, temp, scales, pt_dram, ident, pt):
    with ExitStack() as ctx:
        def sb(name, shape):
            return ctx.enter_context(nc.sbuf_tensor(f"at_{name}", shape, F32))

        def sem(name):
            return ctx.enter_context(nc.semaphore(f"at_{name}"))

        rowq = sb("rowq", [PAIR, NPAIR])
        colk = sb("colk", [PAIR, NPAIR, PAIR])
        tq = sb("tq", [PAIR, NPAIR])
        av = sb("av", [PAIR, len(TOPK)])
        half = sb("half", [PAIR, 2])
        full = sb("full", [PAIR, NPAIR, PAIR])
        lower = sb("lower", [PAIR, NPAIR, HC])
        att = sb("att", [PAIR, NPAIR, HC])
        left = sb("left", [PAIR, len(TOPK), NPAIR, HC])
        top = sb("top", [PAIR, NPAIR, 5, 8])
        nmax = sb("nmax", [PAIR, NPAIR])
        ex = sb("ex", [PAIR, NPAIR, HC])
        kept = sb("kept", [PAIR, len(TOPK), NPAIR, HC])
        total = sb("total", [PAIR, len(TOPK), NPAIR])
        coef = sb("coef", [PAIR, len(TOPK), NPAIR])
        prob = sb("prob", [PAIR, NPAIR, HC])
        wide = sb("wide", [PAIR, NPAIR, PAIR])
        zero = sb("zero", [P, CB, C])
        ptT = sb("ptT", [PAIR, NPAIR, PAIR])
        tps = ctx.enter_context(nc.psum_tensor("at_tps", [P, 512], F32))
        c_in, link, halves, nmax_ready, exp_done, turned, zero_ready, out_done = (
            sem("c_in"), sem("link"), sem("halves"), sem("nmax_ready"), sem("exp_done"), sem("turned"),
            sem("zero_ready"), sem("out_done"))
        wide_ready, ptT_ready, pt_in = sem("wide_ready"), sem("ptT_ready"), sem("pt_in")
        block = ctx.enter_context(nc.Block())

        @block.sync
        def _(sp):
            sp.dma_start(rowq[:, :], rq_dram[0:C].rearrange("(h p) -> p h", p=PAIR),
                         allow_slow_non_contiguous=True).then_inc(c_in, 16)
            sp.dma_start(colk[:, :, :].rearrange("p h n -> p (h n)"),
                         rq_dram[C:2 * C].unsqueeze(0).broadcast_to([PAIR, C])).then_inc(c_in, 16)
            t2 = temp.rearrange("(h two) a b -> two (h a b)", two=2)
            for s in range(2):
                sp.dma_start(tq[s * HC:(s + 1) * HC, :], t2[s:s + 1, :].broadcast_to([HC, NPAIR]),
                             allow_slow_non_contiguous=True).then_inc(c_in, 16)
            for n, a in enumerate(scales):
                sp.dma_start(av[:, n:n + 1], a.unsqueeze(0).broadcast_to([PAIR, 1]),
                             allow_slow_non_contiguous=True).then_inc(c_in, 16)
            sp.wait_ge(zero_ready, 1)
            sp.dma_start(pt_dram.rearrange("(b p) n -> p b n", p=P), zero[:, :, :]).then_inc(out_done, 16)
            sp.wait_ge(out_done, 16)
            sp.wait_ge(ptT_ready, 1)
            for h in range(NPAIR):
                sp.dma_start(pt_dram[h * PAIR:(h + 1) * PAIR, h * PAIR:(h + 1) * PAIR], ptT[:, h, :]).then_inc(out_done, 16)
            sp.wait_ge(out_done, 16 + 16 * NPAIR)
            sp.dma_start(pt[:, :, :], pt_dram.rearrange("(b p) n -> p b n", p=P)).then_inc(pt_in, 16)
            sp.wait_ge(pt_in, 16)

        @block.gpsimd
        def _(gp):
            nc.gpsimd.memset(half[:, :], 1.0).then_inc(halves, 1)
            gp.wait_ge(halves, 1)
            nc.gpsimd.affine_select(half[:, 0:1], half[:, 0:1], [[0, 1]], ALU.is_ge, 0.0,
                                    base=HC - 1, channel_multiplier=-1).then_inc(halves, 1)
            nc.gpsimd.affine_select(half[:, 1:2], half[:, 1:2], [[0, 1]], ALU.is_ge, 0.0,
                                    base=-HC, channel_multiplier=1).then_inc(halves, 1)
            nc.gpsimd.memset(zero[:, :, :], 0.0).then_inc(zero_ready, 1)

        @block.scalar
        def _(act):
            act.wait_ge(nmax_ready, 1)
            for h in range(NPAIR):
                nc.scalar.activation(ex[:, h, :], att[:, h, :], ACT.Exp, bias=nmax[:, h:h + 1]).then_inc(exp_done, 1)

        @block.vector
        def _(dve):
            count = [0]

            def chained(ins):
                count[0] += 1
                ins.then_inc(link, 1)
                dve.wait_ge(link, count[0])

            V = nc.vector
            dve.wait_ge(c_in, 16 * (4 + len(scales)))
            dve.wait_ge(halves, 3)
            chained(V.tensor_tensor(full[:, :, :], gram[0:PAIR, 0:C].rearrange("p (h n) -> p h n", h=NPAIR),
                                    colk[:, :, :], ALU.mult))
            for h in range(NPAIR):
                chained(V.tensor_scalar(full[:, h, :], full[:, h, :], rowq[:, h:h + 1], tq[:, h:h + 1], ALU.mult, ALU.mult))
            chained(V.tensor_scalar(lower[:, :, :], full[:, :, HC:PAIR], half[:, 1:2], None, ALU.mult))
            chained(V.scalar_tensor_tensor(att[:, :, :], full[:, :, 0:HC], half[:, 0:1], lower[:, :, :], ALU.mult, ALU.add))
            rounds = TOPK[1] // 8
            for h in range(NPAIR):
                cur = att[:, h, :]
                for r in range(rounds):
                    chained(V.max(top[:, h, r, :], cur))
                    nxt = left[:, 0, h, :] if (r + 1) * 8 <= TOPK[0] else left[:, 1, h, :]
                    chained(V.match_replace(nxt, top[:, h, r, :], cur, TAKEN))
                    cur = nxt
                for k in (3, 2):
                    chained(V.max(top[:, h, rounds, :], left[:, 1, h, :]))
                    chained(V.memset(top[:, h, rounds, TOPK[k] - TOPK[1]:8], TAKEN))
                    chained(V.match_replace(left[:, k, h, :], top[:, h, rounds, :], left[:, 1, h, :], TAKEN))
            V.tensor_scalar(nmax[:, :], top[:, :, 0, 0], -1.0, None, ALU.mult).then_inc(nmax_ready, 1)
            dve.wait_ge(exp_done, NPAIR)
            for k in range(len(TOPK)):
                for h in range(NPAIR):
                    chained(V.scalar_tensor_tensor(kept[:, k, h, :], left[:, k, h, :], TAKEN, ex[:, h, :],
                                                   ALU.is_equal, ALU.mult))
            chained(V.tensor_reduce(total[:, :, :], kept[:, :, :, :], AX.X, ALU.add))
            chained(V.reciprocal(coef[:, :, :], total[:, :, :]))
            for k in range(len(TOPK)):
                chained(V.tensor_scalar(coef[:, k, :], coef[:, k, :], av[:, k:k + 1], None, ALU.mult))
            for h in range(NPAIR):
                chained(V.tensor_scalar(prob[:, h, :], kept[:, 0, h, :], coef[:, 0, h:h + 1], None, ALU.mult))
                for k in range(1, len(TOPK)):
                    chained(V.scalar_tensor_tensor(prob[:, h, :], kept[:, k, h, :], coef[:, k, h:h + 1], prob[:, h, :],
                                                   ALU.mult, ALU.add))
            V.tensor_scalar(wide[:, :, 0:HC], prob[:, :, :], half[:, 0:1], None, ALU.mult).then_inc(wide_ready, 1)
            V.tensor_scalar(wide[:, :, HC:PAIR], prob[:, :, :], half[:, 1:2], None, ALU.mult).then_inc(wide_ready, 1)
            dve.wait_ge(turned, 1)
            V.tensor_copy(ptT[:, :, :], tps[0:PAIR, 0:C].rearrange("p (h n) -> p h n", h=NPAIR)).then_inc(ptT_ready, 1)

        @block.tensor
        def _(pe):
            pe.wait_ge(wide_ready, 2)
            for h in range(NPAIR):
                ins = nc.tensor.transpose(tps[0:PAIR, h * PAIR:(h + 1) * PAIR], wide[:, h, :], ident[0:PAIR, 0:PAIR])
            ins.then_inc(turned, 1)


def stage_project(nc, x3, v_dram, pt, wpT, b_proj, ident, stats, patch_dram):
    NTR = 4
    runs = [(b, j, min(NTR, TJ - j)) for b in range(CB) for j in range(0, TJ, NTR)]
    NRUN = len(runs)
    RPB = NRUN // CB
    FIRST_REC, REC = 1, 3
    need = [sorted({c // P for h in range(HEADS) if h * HC < (o + 1) * P and (h + 1) * HC > o * P
                    for c in (h * HC, (h + 1) * HC - 1)}) for o in range(CB)]
    with ExitStack() as ctx:
        def sb(name, shape, dt=F32):
            return ctx.enter_context(nc.sbuf_tensor(f"pr_{name}", shape, dt))

        def sem(name):
            return ctx.enter_context(nc.semaphore(f"pr_{name}"))

        vb = sb("vb", [P, 2, CB, PX])
        xb = sb("xb", [P, 2, CB, ROWS, XW])
        ge = sb("ge", [P, CB, PX])
        yb = sb("yb", [P, CB, PR, XW // 2])
        x1 = sb("x1", [P, 2, CB, TJ, TW, TH])
        turned = sb("turned", [P, CB, P, TJ])
        wp = sb("wp", [P, CB, C])
        bp = sb("bp", [P, CB])
        abank = [ctx.enter_context(nc.psum_tensor(f"pr_ab{i}", [P, 512], F32)) for i in range(CB)]
        ybank = [ctx.enter_context(nc.psum_tensor(f"pr_yb{i}", [P, 512], F32)) for i in range(CB)]
        tbank = [ctx.enter_context(nc.psum_tensor(f"pr_tb{i}", [P, 512], F32)) for i in range(2)]
        c_in, zeroed = sem("c_in"), sem("zeroed")
        v_in = [sem("v_in0"), sem("v_in1")]
        x_in = [sem("x_in0"), sem("x_in1")]
        att_done, gelu_done, proj_done, y_ready = sem("att_done"), sem("gelu_done"), sem("proj_done"), sem("y_ready")
        x1_done, st_done = sem("x1_done"), sem("st_done")
        tr_done, tr_out = sem("tr_done"), sem("tr_out")
        stored = [sem(f"stored{b}") for b in range(CB)]
        block = ctx.enter_context(nc.Block())
        src = x3.rearrange("(b p) (y x) -> b p y x", p=P, x=W)
        vsrc = v_dram.rearrange("(b p) n -> p b n", p=P)

        def run(eng, step, head=2, tail=STEPS):
            for t in range(head):
                step(t, t % 2)
            with eng.Fori(head // 2, tail // 2) as i:
                step(i * 2, 0, True)
                step(i * 2 + 1, 1, True)
            for t in range(tail, STEPS + 1):
                step(t, t % 2)

        @block.sync
        def _(sp):
            sp.dma_start(wp[:, :, :], wpT.rearrange("(b p) n -> p b n", p=P)).then_inc(c_in, 16)
            sp.dma_start(bp[:, :], b_proj.rearrange("(b p) -> p b", p=P), allow_slow_non_contiguous=True).then_inc(c_in, 16)

            def load(t, par):
                sp.dma_start(vb[:, par], vsrc[:, :, bass.ds(t * PX + PW, PX)]).then_inc(v_in[par], 16)
                for b in range(CB):
                    sp.dma_start(xb[:, par, b, :, PAD:PAD + W], src[b, :, bass.ds(t * ROWS, ROWS), :]).then_inc(x_in[par], 16)

            sp.wait_ge(zeroed, 4)
            load(0, 0)
            load(1, 1)

            def step(t, par, inner=False):
                if inner or t >= 1:
                    for b in range(CB):
                        address(sp, (t - 1) * (GRP * TJ) + b * (P // GRP) * TI * GRP * TJ)
                        sp.wait_ge(tr_out, t * NRUN - NRUN + (b + 1) * RPB)
                        sp.dma_start(
                            patch_dram[:, b * (P // GRP):(b + 1) * (P // GRP), bass.ds(t - 1, 1), :].rearrange("p g a n -> p g (a n)"),
                            turned[:, b].rearrange("p (g c) j -> p g (c j)", c=GRP)).then_inc(stored[b], 16)
                if inner or t + 2 < STEPS:
                    address(sp, (t + 2) * PX + PW)
                    address(sp, (t + 2) * ROWS * W)
                    if inner:
                        sp.compute_val(t + 1)
                    sp.wait_ge(att_done, t * CB + CB)
                    sp.wait_ge(x1_done, t + 1)
                    load(t + 2, par)

            run(sp, step, tail=STEPS - 2)
            for b in range(CB):
                sp.wait_ge(tr_out, STEPS * NRUN + (b + 1) * RPB)
                sp.dma_start(patch_dram[:, b * (P // GRP):(b + 1) * (P // GRP), STEPS, :],
                             turned[:, b].rearrange("p (g c) j -> p g (c j)", c=GRP)).then_inc(stored[b], 16)
            for b in range(CB):
                sp.wait_ge(stored[b], 16 * (STEPS + 1))

        @block.scalar
        def _(act):
            def evacuate(t):
                for n, (b, j, k) in enumerate(runs):
                    act.wait_ge(tr_done, t * NRUN + n + 1)
                    if n % RPB == 0 and not (at(t, 0)):
                        act.wait_ge(stored[b], t * 16)
                    nc.scalar.activation(turned[:, b, :, j:j + k].rearrange("p c j -> p j c"),
                                         tbank[n % 2][:, 0:k * P].rearrange("p (j c) -> p j c", j=k),
                                         ACT.Copy).then_inc(tr_out, 1)

            def step(t, par, inner=False):
                if inner or t < STEPS:
                    if inner or t >= 1:
                        act.wait_ge(proj_done, t * CB)
                    for o in range(CB):
                        act.wait_ge(att_done, t * CB + o + 1)
                        nc.scalar.activation(ge[:, o, :], abank[o][:, 0:PX], ACT.Gelu).then_inc(gelu_done, 1)
                if inner or t >= 1:
                    evacuate(t - 1)
                if inner or t < STEPS:
                    if inner or t >= 1:
                        act.wait_ge(x1_done, t)
                    else:
                        act.wait_ge(c_in, 32)
                        act.wait_ge(zeroed, 4)
                    for o in range(CB):
                        act.wait_ge(proj_done, t * CB + o + 1)
                        nc.scalar.activation(yb[:, o, :, PAD // 2:PAD // 2 + PW], ybank[o][:, 0:PX].rearrange("p (y x) -> p y x", y=PR), ACT.Identity, bias=bp[:, o:o + 1]).then_inc(y_ready, 1)

            run(act, step)
            evacuate(STEPS)

        @block.vector
        def _(dve):
            nc.vector.memset(xb[:, 0], 0.0).then_inc(zeroed, 1)
            nc.vector.memset(xb[:, 1], 0.0).then_inc(zeroed, 1)
            nc.vector.memset(yb[:, :, :, :], 0.0).then_inc(zeroed, 1)
            nc.vector.memset(x1[:, 0], 0.0).then_inc(zeroed, 1)
            dve.wait_ge(zeroed, 4)

            def add(par, b, buf, y, row, n):
                out = x1[:, buf, b, :, :, row:row + 2 * n - 1:2].rearrange("p j (x c) y -> p y (j x) c", c=2)
                x = xb[:, par, b, y:y + 2 * n - 1:2, :].rearrange("p y (x c) -> p y x c", c=2)
                low = yb[:, b, y // 2:y // 2 + n, :].unsqueeze(3).broadcast_to([P, n, XW // 2, 2])
                return nc.vector.tensor_tensor(out, x, low, ALU.add)

            def record(n, b, pixels):
                return nc.vector.bn_stats(stats[:, b, bass.ds(n, 1), :].rearrange("p a s -> p (a s)"), pixels)

            def step(t, par, inner=False):
                if inner or t < STEPS:
                    dve.wait_ge(x_in[par], (t // 2 + 1) * 16 * CB if isinstance(t, int) else (t - par) * 8 * CB + 16 * CB)
                    if inner or t >= 1:
                        dve.wait_ge(tr_done, t * NRUN)
                        dve.wait_ge(st_done, t)
                    for b in range(CB):
                        dve.wait_ge(y_ready, t * CB + b + 1)
                        for r in range(2):
                            add(par, b, par, r, PAD + r, 1)
                            ins = add(par, b, 1 - par, 2 + r, r, PAD // 2)
                    ins.then_inc(x1_done, 1)
                    dve.wait_ge(x1_done, t + 1)
                    for b in range(CB):
                        flat = x1[:, par, b].rearrange("p j x y -> p (j x) y")[:, PAD:PAD + W, :]
                        if at(t, 0):
                            ins = record(0, b, flat[:, :, PAD:TH])
                        else:
                            for k in range(REC):
                                ins = record(t * REC - REC + FIRST_REC + k, b,
                                             flat[:, k * W // REC:(k + 1) * W // REC, :].rearrange("p x y -> p (x y)"))
                    ins.then_inc(st_done, 1)

            run(dve, step)
            for b in range(CB):
                flat = x1[:, STEPS % 2, b].rearrange("p j x y -> p (j x) y")[:, PAD:PAD + W, :]
                for k in range(REC):
                    ins = record(STEPS * REC - REC + FIRST_REC + k, b, flat[:, k * W // REC:(k + 1) * W // REC, 0:PAD])
            ins.then_inc(st_done, 1)
            dve.wait_ge(st_done, STEPS + 1)

        @block.tensor
        def _(pe):
            pe.wait_ge(c_in, 32)

            def patches(t, par):
                pe.wait_ge(x1_done, STEPS if at(t, STEPS) else t + 1)
                for n, (b, j0, k) in enumerate(runs):
                    if not (at(t, 0) and n < 2):
                        pe.wait_ge(tr_out, t * NRUN + n - 1)
                    for j in range(k):
                        ins = nc.tensor.transpose(
                            tbank[n % 2][:, j * P:(j + 1) * P],
                            x1[:, par, b, j0 + j].rearrange("p x y -> p (x y)"), ident[:, :])
                    ins.then_inc(tr_done, 1)

            def step(t, par, inner=False):
                if inner or t < STEPS:
                    pe.wait_ge(v_in[par], (t // 2) * 16 + 16 if isinstance(t, int) else (t - par) * 8 + 16)
                    for o in range(CB):
                        if inner or t >= 1:
                            pe.wait_ge(gelu_done, t * CB - CB + o + 1)
                        for n, b in enumerate(need[o]):
                            ins = nc.tensor.matmul(abank[o][:, 0:PX], pt[:, b, o * P:(o + 1) * P], vb[:, par, b, :],
                                                   start=n == 0, stop=n == len(need[o]) - 1)
                        ins.then_inc(att_done, 1)
                if inner or t >= 1:
                    patches(t - 1, 1 - par)
                if inner or t < STEPS:
                    pe.wait_ge(gelu_done, t * CB + CB)
                    for o in range(CB):
                        if inner or t >= 1:
                            pe.wait_ge(y_ready, t * CB - CB + o + 1)
                        for b in range(CB):
                            ins = nc.tensor.matmul(ybank[o][:, 0:PX], wp[:, b, o * P:(o + 1) * P], ge[:, b, :],
                                                   start=b == 0, stop=b == CB - 1)
                        ins.then_inc(proj_done, 1)

            run(pe, step)
            patches(STEPS, STEPS % 2)


def stage_kernels(nc, w_large, w_small, norms, mean, rstd, toep_dram, const_dram):
    with ExitStack() as ctx:
        def sb(name, shape, dt=F32):
            return ctx.enter_context(nc.sbuf_tensor(f"kn_{name}", shape, dt))

        def sem(name):
            return ctx.enter_context(nc.semaphore(f"kn_{name}"))

        wl = sb("wl", [P, CB, KL, KL])
        ws = sb("ws", [P, CB, KS, KS])
        bn = sb("bn", [P, 12, CB])
        eps = sb("eps", [P, 1])
        std = sb("std", [P, 3, CB])
        sc = sb("sc", [P, 3, CB])
        sh = sb("sh", [P, 3, CB])
        sc64 = sb("sc64", [P, 3, CB])
        inv = sb("inv", [P, CB])
        cst = sb("cst", [P, CB, 3])
        padw = sb("padw", [P, CB, 2, JR, JX], F16)
        band = sb("band", [P, 3, JR, TW, NU, 2], F16)
        c_in, link, std_done, hi_done, pad_zero, pad_ready = (sem("c_in"), sem("link"), sem("std_done"),
                                                              sem("hi_done"), sem("pad_zero"), sem("pad_ready"))
        made = [sem("made0"), sem("made1"), sem("made2")]
        sent = [sem("sent0"), sem("sent1"), sem("sent2")]
        cst_ready, cst_out = sem("cst_ready"), sem("cst_out")
        block = ctx.enter_context(nc.Block())
        jobs = [(b, ix) for b in range(CB) for ix in range(TW)]

        def make(eng, who, copy):
            eng.wait_ge(pad_ready, 1)
            for n, (b, ix) in enumerate(jobs):
                if n % 3 != who:
                    continue
                if n >= 3:
                    eng.wait_ge(sent[who], 16 * (n // 3))
                for part in range(2):
                    win = bass.AP(padw, ((b * 2 + part) * JR) * JX + ix,
                                  [[CB * 2 * JR * JX, P], [TW, NU], [JX, JR], [1, TW]])
                    copy(band[:, who, :, :, :, part].rearrange("p j x u -> p u j x"), win).then_inc(made[who], 1)

        @block.sync
        def _(sp):
            sp.dma_start(wl[:, :, :, :], w_large.rearrange("(b p) o y x -> p b (o y) x", p=P)).then_inc(c_in, 16)
            sp.dma_start(ws[:, :, :, :], w_small.rearrange("(b p) o y x -> p b (o y) x", p=P)).then_inc(c_in, 16)
            for n, a in enumerate(norms):
                sp.dma_start(bn[:, n, :], a.rearrange("(b p) -> p b", p=P), allow_slow_non_contiguous=True).then_inc(c_in, 16)
            for n, (b, ix) in enumerate(jobs):
                w = n % 3
                sp.wait_ge(made[w], 2 * (n // 3 + 1))
                sp.dma_start(toep_dram[b * P:(b + 1) * P, ix, :],
                             band[:, w].rearrange("p j x u a -> p (j x u a)")).then_inc(sent[w], 16)
            sp.wait_ge(cst_ready, 1)
            sp.dma_start(const_dram.rearrange("(b p) s -> p b s", p=P), cst[:, :, :],
                         allow_slow_non_contiguous=True).then_inc(cst_out, 16)
            for w in range(3):
                sp.wait_ge(sent[w], 16 * (len(jobs) // 3))
            sp.wait_ge(cst_out, 16)

        @block.scalar
        def _(act):
            act.wait_ge(link, 1)
            act.wait_ge(c_in, 16 * 14)
            for k in range(3):
                nc.scalar.activation(std[:, k, :], bn[:, 4 * k + 3, :], ACT.Sqrt, bias=eps[:, :]).then_inc(std_done, 1)
            make(act, 1, lambda o, i: nc.scalar.activation(o, i, ACT.Copy))

        @block.gpsimd
        def _(gp):
            nc.gpsimd.memset(padw[:, :, :, :, :], 0.0).then_inc(pad_zero, 1)
            make(gp, 2, nc.gpsimd.tensor_copy)

        @block.vector
        def _(dve):
            V = nc.vector
            count = [0]

            def chained(ins):
                count[0] += 1
                ins.then_inc(link, 1)
                dve.wait_ge(link, count[0])

            chained(V.memset(eps[:, :], 1e-5))
            dve.wait_ge(std_done, 3)
            chained(V.reciprocal(std[:, :, :], std[:, :, :]))
            for k in range(3):
                chained(V.tensor_tensor(sc[:, k, :], std[:, k, :], bn[:, 4 * k, :], ALU.mult))
                chained(V.tensor_tensor(sh[:, k, :], sc[:, k, :], bn[:, 4 * k + 2, :], ALU.mult))
                chained(V.tensor_tensor(sh[:, k, :], bn[:, 4 * k + 1, :], sh[:, k, :], ALU.subtract))
            chained(V.reciprocal(inv[:, :], rstd[:, :]))
            chained(V.tensor_tensor(inv[:, :], inv[:, :], sc[:, 2, :], ALU.add))
            chained(V.tensor_scalar(sc64[:, 0:2, :], sc[:, 0:2, :], SCALE, None, ALU.mult))
            chained(V.tensor_scalar(sc64[:, 2, :], inv[:, :], SCALE, None, ALU.mult))
            mid = KL // 2
            for b in range(CB):
                flat = wl[:, b].rearrange("p y x -> p (y x)")
                chained(V.tensor_scalar(flat, flat, sc64[:, 0, b:b + 1], None, ALU.mult))
                inner = wl[:, b, mid - 1:mid + 2, mid - 1:mid + 2]
                chained(V.scalar_tensor_tensor(inner, ws[:, b], sc64[:, 1, b:b + 1], inner, ALU.mult, ALU.add))
                centre = wl[:, b, mid, mid:mid + 1]
                chained(V.tensor_tensor(centre, centre, sc64[:, 2, b:b + 1], ALU.add))
            dve.wait_ge(pad_zero, 1)
            parts = [padw[:, :, k, TH - 1:TH - 1 + KL, TW - 1:TW - 1 + KL] for k in range(2)]
            for b in range(CB):
                chained(V.tensor_copy(parts[0][:, b], wl[:, b]))
            for b in range(CB):
                chained(V.tensor_tensor(parts[1][:, b], wl[:, b], parts[0][:, b], ALU.subtract))
            dve.sem_inc(pad_ready, 1)
            chained(V.tensor_copy(cst[:, :, 0], mean[:, :]))
            chained(V.tensor_scalar(cst[:, :, 1], rstd[:, :], SCALE, None, ALU.mult))
            chained(V.tensor_tensor(cst[:, :, 2], mean[:, :], sh[:, 0, :], ALU.add))
            chained(V.tensor_tensor(cst[:, :, 2], cst[:, :, 2], sh[:, 1, :], ALU.add))
            V.tensor_tensor(cst[:, :, 2], cst[:, :, 2], sh[:, 2, :], ALU.add).then_inc(cst_ready, 1)
            make(dve, 0, V.tensor_copy)


def stage_depthwise(nc, patch_dram, toep_dram, const_dram, ident, out3):
    NTOEP = 8
    NCB = 4
    NBB = 3
    TPB = 4
    FILLS = NBAND * OJ // TPB
    NPIX = OI * OJ
    with ExitStack() as ctx:
        def sb(name, shape, dt=F32):
            return ctx.enter_context(nc.sbuf_tensor(f"cv_{name}", shape, dt))

        def sem(name):
            return ctx.enter_context(nc.semaphore(f"cv_{name}"))

        raw = sb("raw", [P, 2, TI, GRP, TJ])
        hi = sb("hi", [P, 2, TI, GRP, TJ], F16)
        lo = sb("lo", [P, 2, TI, GRP, TJ], F16)
        cst = sb("cst", [P, C, 3])
        toep = sb("toep", [P, NTOEP, KRUN], F16)
        res = sb("res", [P, 2, NBAND, OJ, GRP, BAND])
        rows = sb("rows", [P, NBAND, TH, W])
        side = sb("side", [P, 4])
        rowsel = sb("rowsel", [P, TW])
        cbank = [ctx.enter_context(nc.psum_tensor(f"cv_cb{i}", [P, 512], F32)) for i in range(NCB)]
        bbank = [ctx.enter_context(nc.psum_tensor(f"cv_bb{i}", [P, 512], F32)) for i in range(NBB)]
        raw_in, cst_in = [sem("raw_in0"), sem("raw_in1")], sem("cst_in")
        toep_in = [sem(f"toep_in{i}") for i in range(NTOEP)]
        side_ready = sem("side_ready")
        masks, norm_done, edge_done, hi_done, lo_done = (sem("masks"), sem("norm_done"), sem("edge_done"),
                                                         sem("hi_done"), sem("lo_done"))
        conv_done, res_done, back_done, rows_done = (sem("conv_done"), sem("res_done"), sem("back_done"),
                                                     sem("rows_done"))
        out_done = [sem(f"out_done{i}") for i in range(NBAND)]
        block = ctx.enter_context(nc.Block())
        shift = [(s, u) for s in range(NS) for u in range(NU)]

        def run(eng, step, tail=NG):
            step(0, 0)
            step(1, 1)
            with eng.Fori(1, tail // 2) as i:
                step(i * 2, 0, True)
                step(i * 2 + 1, 1, True)
            for g in range(tail, NG + 1):
                step(g, g % 2)

        @block.sync
        def _(sp):
            def load_group(g, par):
                sp.dma_start(raw[:, par].rearrange("p i c j -> p (i c j)"),
                             patch_dram[:, bass.ds(g, 1), :, :].rearrange("p a i n -> p (a i n)")).then_inc(raw_in[par], 16)

            sp.dma_start(cst[:, :, :].rearrange("p c s -> p (c s)"),
                         const_dram.rearrange("c s -> (c s)").unsqueeze(0).broadcast_to([P, C * 3])).then_inc(cst_in, 16)
            load_group(0, 0)
            load_group(1, 1)

            def step(g, par, inner=False):
                for c in range(GRP):
                    if c == GRP // 2 and (inner or g + 2 < NG):
                        address(sp, (g + 2) * (TI * GRP * TJ))
                        sp.wait_ge(lo_done, g + 1)
                        load_group(g + 2, par)
                    if inner or g < NG:
                        address(sp, (g * GRP + c) * (TW * JR * TW * NU * 2), 2)
                        if inner or g * GRP + c >= NTOEP:
                            sp.wait_ge(conv_done, g * GRP + c - NTOEP + 1)
                        sp.dma_start(toep[:, c % NTOEP],
                                     toep_rows(g * GRP + c)).then_inc(toep_in[c % NTOEP], 16)

            def toep_rows(ch):
                v = toep_dram[bass.ds(ch, 1), :, :].rearrange("a i n -> (a i) n")
                return bass.AP(v.tensor, v.offset, [[JR * TW * NU * 2, TW], [TW * NU * 2, TH], [1, KRUN]])

            run(sp, step, tail=NG - 2)

        @block.gpsimd
        def _(gp):
            nc.gpsimd.memset(side[:, :], 1.0).then_inc(masks, 1)
            gp.wait_ge(masks, 1)
            nc.gpsimd.affine_select(side[:, 0:1], side[:, 0:1], [[0, 1]], ALU.is_ge, 0.0,
                                    base=-PAD * TH, channel_multiplier=1).then_inc(masks, 1)
            nc.gpsimd.affine_select(side[:, 1:2], side[:, 1:2], [[0, 1]], ALU.is_ge, 0.0,
                                    base=PAD * TH - 1, channel_multiplier=-1).then_inc(masks, 1)
            nc.gpsimd.memset(rowsel[:, :], 1.0).then_inc(masks, 1)
            gp.wait_ge(masks, 4)
            nc.gpsimd.affine_select(rowsel[:, :], rowsel[:, :], [[-TH, TW]], ALU.is_ge, 0.0,
                                    base=-PAD, channel_multiplier=1).then_inc(masks, 1)
            gp.wait_ge(masks, 5)
            nc.gpsimd.affine_select(rowsel[:, :], rowsel[:, :], [[TH, TW]], ALU.is_ge, 0.0,
                                    base=TH - 1, channel_multiplier=-1).then_inc(masks, 1)

        @block.scalar
        def _(act):
            STORE_AT = (7, 10, 13)

            def store(g, bd):
                act.wait_ge(rows_done, g * FILLS + (bd + 1) * (FILLS // NBAND))
                act.dma_start(out3[bass.ds(g * GRP, GRP), bd * BAND * TH * W:(bd + 1) * BAND * TH * W]
                              .rearrange("c (t n) -> c t n", t=BAND),
                              rows[:, bd].rearrange("p y x -> p (y x)")).then_inc(out_done[bd], 16)

            act.wait_ge(cst_in, 16)

            def split(g, par):
                act.wait_ge(edge_done, g + 1)
                if not (isinstance(g, int) and g < 2):
                    act.wait_ge(conv_done, g * GRP - GRP)
                nc.scalar.activation(hi[:, par], raw[:, par], ACT.Copy).then_inc(hi_done, 1)

            split(0, 0)

            def step(g, par, inner=False):
                if not inner and g >= NG:
                    for bd in range(NBAND):
                        store(g - 1, bd)
                    return
                if inner or g >= 2:
                    act.wait_ge(back_done, g * FILLS - FILLS)
                for c in range(GRP):
                    if (inner or g >= 1) and c in STORE_AT:
                        store(g - 1, STORE_AT.index(c))
                    act.wait_ge(conv_done, g * GRP + c + 1)
                    nc.scalar.activation(res[:, par, :, :, c, :],
                                         cbank[c % NCB][:, 0:NPIX].rearrange("p (b i j) -> p b j i", b=NBAND, j=OJ),
                                         ACT.Identity, bias=cst[:, bass.ds(g * GRP + c, 1), 2], scale=UNSCALE).then_inc(res_done, 1)
                    if c == GRP // 4 and (inner or g + 1 < NG):
                        split(g + 1, 1 - par)

            run(act, step, tail=NG - 2)
            for bd in range(NBAND):
                act.wait_ge(out_done[bd], 16 * NG)

        @block.vector
        def _(dve):
            V = nc.vector
            EDGES = 4
            dve.wait_ge(masks, 6)
            V.tensor_reduce(side[:, 2:3], rowsel[:, :], AX.X, ALU.add).then_inc(side_ready, 1)
            dve.wait_ge(side_ready, 1)
            V.tensor_scalar(side[:, 3:4], side[:, 2:3], -1.0, 1.0, ALU.mult, ALU.add).then_inc(side_ready, 1)
            dve.wait_ge(side_ready, 2)
            dve.wait_ge(cst_in, 16)

            def normalise(g, par):
                dve.wait_ge(raw_in[par], (g // 2) * 16 + 16 if isinstance(g, int) else (g - par) * 8 + 16)
                for c in range(GRP):
                    V.tensor_scalar(raw[:, par, :, c, :], raw[:, par, :, c, :],
                                    cst[:, bass.ds(g * GRP + c, 1), 0], cst[:, bass.ds(g * GRP + c, 1), 1],
                                    ALU.subtract, ALU.mult).then_inc(norm_done, 1)
                dve.wait_ge(norm_done, g * (GRP + EDGES - 1) + GRP)
                flat = raw[:, par].rearrange("p i c j -> p (i c) j")
                edges = [(flat[:, :, 0], 0), (flat[:, :, TJ - 1], 1),
                         (raw[:, par, 0].rearrange("p c j -> p (c j)"), 2), (raw[:, par, TI - 1].rearrange("p c j -> p (c j)"), 3)]
                for n, (e, m) in enumerate(edges):
                    ins = V.tensor_scalar(e, e, side[:, m:m + 1], None, ALU.mult)
                    if n < EDGES - 1:
                        ins.then_inc(norm_done, 1)
                        dve.wait_ge(norm_done, g * (GRP + EDGES - 1) + GRP + n + 1)
                    else:
                        ins.then_inc(edge_done, 1)

            def low(g, par):
                dve.wait_ge(hi_done, g + 1)
                dve.wait_ge(edge_done, g + 1)
                if not (isinstance(g, int) and g < 2):
                    dve.wait_ge(conv_done, g * GRP - GRP)
                V.tensor_tensor(lo[:, par].rearrange("p i c j -> p (i c j)"), raw[:, par].rearrange("p i c j -> p (i c j)"),
                                hi[:, par].rearrange("p i c j -> p (i c j)"), ALU.subtract).then_inc(lo_done, 1)

            def bring(g, n):
                dve.wait_ge(back_done, g * FILLS + n + 1)
                bd, q = n // (FILLS // NBAND), n % (FILLS // NBAND)
                if n % (FILLS // NBAND) == 0 and not (at(g, 0)):
                    dve.wait_ge(out_done[bd], g * 16)
                src = bbank[n % NBB][:, :].rearrange("p (t y x) -> p t y x", t=TPB, y=TH)[:, :, ::-1, ::-1]
                dst = rows[:, bd, :, q * TPB * TW:(q + 1) * TPB * TW].rearrange("p y (t x) -> p t y x", t=TPB)
                V.tensor_copy(dst, src).then_inc(rows_done, 1)

            normalise(0, 0)
            low(0, 0)

            def step(g, par, inner=False):
                back = inner or g >= 1
                more = inner or g + 1 < NG
                if more:
                    normalise(g + 1, 1 - par)
                for n in range(FILLS):
                    if back:
                        bring(g - 1, n)
                    if n == 3 and more:
                        low(g + 1, 1 - par)

            run(dve, step, tail=NG - 2)

        @block.tensor
        def _(pe):
            FIRST_BACK = 2

            def back(g, par, n):
                if not (at(g, 0) and n < NBB):
                    pe.wait_ge(rows_done, g * FILLS + n - NBB + 1)
                bd, q = n // (FILLS // NBAND), n % (FILLS // NBAND)
                for k in range(TPB):
                    ins = nc.tensor.transpose(bbank[n % NBB][:, k * P:(k + 1) * P],
                                              res[:, par, bd, q * TPB + k].rearrange("p c i -> p (c i)"), ident[:, :])
                ins.then_inc(back_done, 1)

            def step(g, par, inner=False):
                live = inner or g < NG
                if live:
                    pe.wait_ge(lo_done, g + 1)
                for c in range(GRP):
                    if live:
                        rnd = c // NTOEP
                        pe.wait_ge(toep_in[c % NTOEP], g * (16 * GRP // NTOEP) + 16 * (rnd + 1))
                        if inner or g >= 1 or c >= NCB:
                            pe.wait_ge(res_done, g * GRP + c - NCB + 1)
                        n = 0
                        for s, u in shift:
                            rows_in = min(OI, TI - s)
                            out = cbank[c % NCB][:, 0:rows_in * OJ].rearrange("p (i j) -> p i j", j=OJ)
                            for part, x in ((0, hi), (0, lo), (1, hi)):
                                ins = nc.tensor.matmul(
                                    out, toep[:, c % NTOEP, :].rearrange("p (s m v) -> p s v m", s=NS, m=P)[:, s, u * 2 + part],
                                    x[:, par, s:s + rows_in, c, u:u + OJ],
                                    start=n == 0, stop=n == 3 * len(shift) - 1, skip_group_check=True)
                                n += 1
                        ins.then_inc(conv_done, 1)
                    f = c - FIRST_BACK
                    if (inner or g >= 1) and 0 <= f < FILLS:
                        if f == 0:
                            pe.wait_ge(res_done, g * GRP)
                        back(g - 1, 1 - par, f)

            run(pe, step)


def mk_conv_kernel(nc, a, out):
    x3 = a["x"].rearrange("a c h w -> (a c) (h w)")
    out3 = out.rearrange("a c h w -> (a c) (h w)")
    chan_dram = nc.dram_tensor("chan_scratch", [C, 2], F32).ap()
    group_dram = nc.dram_tensor("group_scratch", [C, 2], F32).ap()
    rq_dram = nc.dram_tensor("norm_scratch", [2 * C], F32).ap()
    v_dram = nc.dram_tensor("v_scratch", [C, VROWS * PW], F32).ap()
    pt_dram = nc.dram_tensor("attention_scratch", [C, C], F32).ap()
    patch_dram = nc.dram_tensor("patch_scratch", [P, NG, TI, GRP * TJ], F32).ap()
    toep_dram = nc.dram_tensor("toeplitz_scratch", [C, TW, 2 * NU * JR * TW], F16).ap()
    const_dram = nc.dram_tensor("constant_scratch", [C, 3], F32).ap()
    with ExitStack() as ctx:
        def sb(name, shape):
            return ctx.enter_context(nc.sbuf_tensor(name, shape, F32))

        ident = sb("ident", [P, P])
        mean, rstd = sb("mean", [P, CB]), sb("rstd", [P, CB])
        pt = sb("pt", [P, CB, C])
        REC0, REC1 = STEPS * (CHUNK // 512), STEPS * 3 + 1
        stats = sb("stats", [P, CB, REC1, 6])
        made = ctx.enter_context(nc.semaphore("ident_made"))
        with nc.Block() as block:
            @block.gpsimd
            def _(gp):
                nc.gpsimd.memset(ident[:, :], 0.0).then_inc(made, 1)
                gp.wait_ge(made, 1)
                nc.gpsimd.affine_select(ident[:, :], ident[:, :], [[-1, P]], ALU.not_equal, 1.0,
                                        base=0, channel_multiplier=1).then_inc(made, 1)
                gp.wait_ge(made, 2)

        stage_statistics(nc, x3, stats[:, :, 0:REC0, :])
        group_affine(nc, "g0", stats[:, :, 0:REC0, :], REC0, chan_dram, group_dram, mean, rstd)
        with nc.psum_tensor("gram", [P, 512], F32) as gram:
            stage_qkv(nc, x3, a["w_qkv_T"], a["b_qkv"], a["w_dw"], a["b_dw"], mean, rstd, ident, rq_dram, v_dram, gram)
            stage_attention(nc, gram, rq_dram, a["temperature"], [a["a1"], a["a2"], a["a3"], a["a4"]], pt_dram, ident, pt)
        stage_project(nc, x3, v_dram, pt, a["w_proj_T"], a["b_proj"], ident, stats, patch_dram)
        group_affine(nc, "g1", stats[:, :, :, :], 0, chan_dram, group_dram, mean, rstd)
        norms = [a[f"{n}_{k}"] for k in "lsi" for n in "gbmv"]
        stage_kernels(nc, a["w_large"], a["w_small"], norms, mean, rstd, toep_dram, const_dram)
        stage_depthwise(nc, patch_dram, toep_dram, const_dram, ident, out3)


def kernel(**inputs):
    import numpy as np
    import concourse.bacc as bacc
    from concourse import mybir as mb
    from concourse.bass_utils import run_bass_kernel_spmd

    nc = bacc.Bacc("TRN2", target_bir_lowering=False, num_devices=1)
    arrays, handles = {}, {}
    for name, value in inputs.items():
        short = name.split("conv_")[-1]
        value = np.asarray(value)
        if short in ("w_qkv", "w_proj"):
            short, value = short + "_T", value.T
        value = np.ascontiguousarray(value)
        arrays[f"in_{short}"] = value
        handles[short] = nc.dram_tensor(f"in_{short}", value.shape, mb.dt.from_np(value.dtype), kind="ExternalInput").ap()
    out = nc.dram_tensor("out_0", (1, C, H, W), F32, kind="ExternalOutput").ap()
    mk_conv_kernel(nc, handles, out)
    result = run_bass_kernel_spmd(nc, [arrays], core_ids=[0])
    return result.results[0]["out_0"]
```

```python
from contextlib import ExitStack

import concourse.bass as bass
from concourse import mybir

ALU = mybir.AluOpType
ACT = mybir.ActivationFunctionType
AX = mybir.AxisListType
F32 = mybir.dt.float32
F16 = mybir.dt.float16

P = 128
C = 384
CB = C // P
H = W = 192
GROUPS = 32
GC = C // GROUPS
ROWS = 8
STEPS = H // ROWS
CHUNK = ROWS * W
QO = 3 * C // P
PR = ROWS // 2
PW = W // 2
PX = PR * PW
VROWS = H // 2 + 1
HEADS = 8
HC = C // HEADS
PAIR = 2 * HC
NPAIR = C // PAIR
TOPK = (HC // 2, HC * 2 // 3, HC * 3 // 4, HC * 4 // 5)
TAKEN = -3.0e38
SCALE = 64.0
UNSCALE = 1.0 / (SCALE * SCALE)

KL = 13
PAD = KL // 2
KS = 3
TH, TW = 8, 16
TI = H // TH + 1
TJ = W // TW + 1
OI, OJ = H // TH, W // TW
NS, NU = 3, 2
XW = TJ * TW
GRP = 16
NG = C // GRP
JR = NS * TH + TH - 1
JX = NU * TW + TW - 1
TCH = TI * GRP * TJ
BAND = P // GRP
NBAND = OI // BAND
KRUN = NS * TH * TW * NU * 2


class Shared:
    pass


def at(step, n):
    return isinstance(step, int) and step == n


def address(eng, elements, size=4):
    if not isinstance(elements, int):
        eng.compute_val(elements * size)
    return elements


def group_affine(nc, tag, stats, member, mean, rstd, ahead=None):
    with ExitStack() as ctx:
        def sb(name, shape):
            return ctx.enter_context(nc.sbuf_tensor(f"{tag}_{name}", shape, F32))

        def sem(name):
            return ctx.enter_context(nc.semaphore(f"{tag}_{name}"))

        chan = sb("chan", [P, CB, 2])
        dev = sb("dev", [P, CB])
        std = sb("std", [P, CB])
        eps = sb("eps", [P, 1])
        avg = ctx.enter_context(nc.psum_tensor(f"{tag}_avg", [P, 512], F32))
        var = ctx.enter_context(nc.psum_tensor(f"{tag}_var", [P, 512], F32))
        link, chan_ready, avg_done, dev_ready, var_done, std_ready = (
            sem("link"), sem("chan_ready"), sem("avg_done"), sem("dev_ready"), sem("var_done"), sem("std_ready"))
        block = ctx.enter_context(nc.Block())

        if ahead is not None:
            block.sync(ahead.first_load)
            block.gpsimd(ahead.masks)

        @block.tensor
        def _(pe):
            pe.wait_ge(chan_ready, CB)
            for o in range(CB):
                for b in range(CB):
                    ins = nc.tensor.matmul(avg[:, o:o + 1], member[:, b, o * P:(o + 1) * P], chan[:, b, 0:1],
                                           start=b == 0, stop=b == CB - 1)
            ins.then_inc(avg_done, 1)
            pe.wait_ge(dev_ready, 1)
            for o in range(CB):
                for b in range(CB):
                    ins = nc.tensor.matmul(var[:, o:o + 1], member[:, b, o * P:(o + 1) * P], dev[:, b:b + 1],
                                           start=b == 0, stop=b == CB - 1)
            ins.then_inc(var_done, 1)

        @block.scalar
        def _(act):
            act.wait_ge(link, 1)
            act.wait_ge(var_done, 1)
            nc.scalar.activation(std[:, :], var[:, 0:CB], ACT.Sqrt, bias=eps[:, :]).then_inc(std_ready, 1)

        @block.vector
        def _(dve):
            V = nc.vector
            count = [0]

            def chained(ins):
                count[0] += 1
                ins.then_inc(link, 1)
                dve.wait_ge(link, count[0])

            chained(V.memset(eps[:, :], 1e-5))
            for b in range(CB):
                V.bn_aggr(chan[:, b, :], stats[:, b, :, :].rearrange("p n s -> p (n s)")).then_inc(chan_ready, 1)
            dve.wait_ge(chan_ready, CB)
            dve.wait_ge(avg_done, 1)
            chained(V.tensor_copy(mean[:, :], avg[:, 0:CB]))
            chained(V.tensor_tensor(dev[:, :], chan[:, :, 0], mean[:, :], ALU.subtract))
            chained(V.tensor_tensor(dev[:, :], dev[:, :], dev[:, :], ALU.mult))
            V.tensor_tensor(dev[:, :], dev[:, :], chan[:, :, 1], ALU.add).then_inc(dev_ready, 1)
            dve.wait_ge(std_ready, 1)
            chained(V.reciprocal(rstd[:, :], std[:, :]))


def stage_statistics(nc, x3, stats, wT, whi, wlo, w_large, w_small, norms, kern, scale, shift, ident, member):
    XBUFS = 4
    REC = CHUNK // 512
    with ExitStack() as ctx:
        xs = ctx.enter_context(nc.sbuf_tensor("st_x", [P, XBUFS, CB, CHUNK], F32))
        x_in = [ctx.enter_context(nc.semaphore(f"st_x_in{i}")) for i in range(XBUFS)]
        x_used = ctx.enter_context(nc.semaphore("st_x_used"))

        def sb(name, shape):
            return ctx.enter_context(nc.sbuf_tensor(f"st_{name}", shape, F32))

        def sem(name):
            return ctx.enter_context(nc.semaphore(f"st_{name}"))

        wst = sb("wst", [P, CB, 3 * C])
        ws = sb("ws", [P, CB, KS, KS])
        bn = sb("bn", [P, 12, CB])
        eps = sb("eps", [P, 1])
        std = sb("std", [P, 3, CB])
        sc64 = sb("sc64", [P, 2, CB])
        made = sem("made")
        w_in, c_in, whi_ready, eps_ready, std_done, link = (sem("w_in"), sem("c_in"), sem("whi_ready"), sem("eps_ready"),
                                                            sem("std_done"), sem("link"))
        block = ctx.enter_context(nc.Block())
        src = x3.rearrange("(b p) n -> p b n", p=P)

        @block.sync
        def _(sp):
            for i in range(XBUFS):
                sp.dma_start(xs[:, i], src[:, :, i * CHUNK:(i + 1) * CHUNK]).then_inc(x_in[i], 16)
            sp.dma_start(wst[:, :, :], wT.rearrange("(b p) n -> p b n", p=P)).then_inc(w_in, 16)
            sp.dma_start(kern[:, :, :, :], w_large.rearrange("(b p) o y x -> p b (o y) x", p=P)).then_inc(c_in, 16)
            sp.dma_start(ws[:, :, :, :], w_small.rearrange("(b p) o y x -> p b (o y) x", p=P)).then_inc(c_in, 16)
            for n, a in enumerate(norms):
                sp.dma_start(bn[:, n, :], a.rearrange("(b p) -> p b", p=P), allow_slow_non_contiguous=True).then_inc(c_in, 16)
            with sp.Fori(1, STEPS // XBUFS) as r:
                for i in range(XBUFS):
                    address(sp, (r * XBUFS + i) * CHUNK)
                    sp.wait_ge(x_used, r * XBUFS + i - XBUFS + 1)
                    sp.dma_start(xs[:, i], src[:, :, bass.ds((r * XBUFS + i) * CHUNK, CHUNK)]).then_inc(x_in[i], 16)

        @block.gpsimd
        def _(gp):
            nc.gpsimd.memset(ident[:, :], 0.0).then_inc(made, 1)
            gp.wait_ge(made, 1)
            nc.gpsimd.affine_select(ident[:, :], ident[:, :], [[-1, P]], ALU.not_equal, 1.0,
                                    base=0, channel_multiplier=1).then_inc(made, 1)
            nc.gpsimd.memset(member[:, :, :], 1.0 / GC).then_inc(made, 1)
            gp.wait_ge(made, 3)
            for b in range(CB):
                view = member[:, b, :].rearrange("p (g k) -> p g k", k=GC)
                nc.gpsimd.affine_select(view, view, [[-GC, GROUPS], [0, GC]], ALU.is_ge, 0.0,
                                        base=b * P, channel_multiplier=1).then_inc(made, 1)
            gp.wait_ge(made, 3 + CB)
            for b in range(CB):
                view = member[:, b, :].rearrange("p (g k) -> p g k", k=GC)
                nc.gpsimd.affine_select(view, view, [[GC, GROUPS], [0, GC]], ALU.is_ge, 0.0,
                                        base=GC - 1 - b * P, channel_multiplier=-1).then_inc(made, 1)
            gp.wait_ge(made, 3 + 2 * CB)

        @block.scalar
        def _(act):
            act.wait_ge(w_in, 16)
            nc.scalar.activation(whi[:, :, :], wst[:, :, :], ACT.Copy, scale=SCALE).then_inc(whi_ready, 1)
            act.wait_ge(eps_ready, 1)
            act.wait_ge(c_in, 16 * 14)
            for k in range(3):
                nc.scalar.activation(std[:, k, :], bn[:, 4 * k + 3, :], ACT.Sqrt, bias=eps[:, :]).then_inc(std_done, 1)

        @block.vector
        def _(dve):
            V = nc.vector
            count = [0]

            def chained(ins):
                count[0] += 1
                ins.then_inc(link, 1)
                dve.wait_ge(link, count[0])

            def statistics(r):
                for i in range(XBUFS):
                    dve.wait_ge(x_in[i], r * 16 + 16)
                    for b in range(CB):
                        for k in range(REC):
                            ins = V.bn_stats(
                                stats[:, b, bass.ds((r * XBUFS + i) * REC + k, 1), :].rearrange("p a s -> p (a s)"),
                                xs[:, i, b, k * 512:(k + 1) * 512])
                    ins.then_inc(x_used, 1)

            V.memset(eps[:, :], 1e-5).then_inc(eps_ready, 1)
            statistics(0)
            dve.wait_ge(whi_ready, 1)
            V.scalar_tensor_tensor(wlo[:, :, :].rearrange("p b n -> p (b n)"), wst[:, :, :].rearrange("p b n -> p (b n)"),
                                   SCALE, whi[:, :, :].rearrange("p b n -> p (b n)"), ALU.mult, ALU.subtract)
            dve.wait_ge(c_in, 16 * 14)
            dve.wait_ge(std_done, 3)
            chained(V.reciprocal(std[:, :, :], std[:, :, :]))
            for k in range(3):
                chained(V.tensor_tensor(scale[:, k, :], std[:, k, :], bn[:, 4 * k, :], ALU.mult))
                chained(V.tensor_tensor(shift[:, k, :], scale[:, k, :], bn[:, 4 * k + 2, :], ALU.mult))
                chained(V.tensor_tensor(shift[:, k, :], bn[:, 4 * k + 1, :], shift[:, k, :], ALU.subtract))
            chained(V.tensor_scalar(sc64[:, :, :], scale[:, 0:2, :], SCALE, None, ALU.mult))
            mid = KL // 2
            for b in range(CB):
                flat = kern[:, b].rearrange("p y x -> p (y x)")
                chained(V.tensor_scalar(flat, flat, sc64[:, 0, b:b + 1], None, ALU.mult))
                inner = kern[:, b, mid - 1:mid + 2, mid - 1:mid + 2]
                chained(V.scalar_tensor_tensor(inner, ws[:, b], sc64[:, 1, b:b + 1], inner, ALU.mult, ALU.add))
            with dve.Fori(1, STEPS // XBUFS) as r:
                statistics(r)


def stage_qkv(nc, x3, whi, wlo, b_qkv, w_dw, b_dw, mean, rstd, ident, kern, rq_dram, v_dram, toep_dram, gram):
    UNITS = STEPS + 1
    NQB = 4
    NTB = 3
    PASSES = 3
    GPS = PR * QO
    QK = 2 * CB
    NTP = PX // P
    NT = 2 * NTP
    TAPS = KS * KS
    with ExitStack() as ctx:
        def sb(name, shape, dt=F32):
            return ctx.enter_context(nc.sbuf_tensor(f"qk_{name}", shape, dt))

        def ps(name, shape):
            return ctx.enter_context(nc.psum_tensor(f"qk_{name}", shape, F32))

        def sem(name):
            return ctx.enter_context(nc.semaphore(f"qk_{name}"))

        xf = sb("xf", [P, 2, CB, CHUNK])
        xhi = sb("xhi", [P, 2, CB, CHUNK], F16)
        xlo = sb("xlo", [P, 2, CB, CHUNK], F16)
        padw = sb("padw", [P, CB, 2, JR, JX], F16)
        band = sb("band", [P, CB, JR, TW, NU, 2], F16)
        pool = sb("pool", [P, 2, QO, PR + 2, PW + 2])
        dw = sb("dw", [P, 2, QO, PX])
        pixT = sb("pixT", [P, NTP, 2, C])
        sq = sb("sq", [P, PX])
        bq = sb("bq", [P, QO])
        bd = sb("bd", [P, QO])
        wd = sb("wd", [P, QO, TAPS])
        sx = sb("sx", [P, CB])
        bx = sb("bx", [P, CB])
        nrm = sb("nrm", [P, QK, UNITS])
        tot = sb("tot", [P, 3, QK])
        qbank = [ps(f"qb{i}", [P, 512]) for i in range(NQB)]
        tbank = [ps(f"tb{i}", [P, 512]) for i in range(NTB)]

        c_in = sem("c_in")
        x_in = [sem("x_in0"), sem("x_in1")]
        prep, zeroed = sem("prep"), sem("zeroed")
        pad_made, band_made, band_out = sem("pad_made"), sem("band_made"), [sem(f"band_out{b}") for b in range(CB)]
        norm_ready, hi_ready, lo_ready = sem("norm_ready"), sem("hi_ready"), sem("lo_ready")
        qkv_done, max_done = sem("qkv_done"), sem("max_done")
        bias_done, halo_done, tap0_done = sem("bias_done"), sem("halo_done"), sem("tap0_done")
        taps_done, dw_done, below_zero = sem("taps_done"), sem("dw_done"), sem("below_zero")
        tr_done, tr_out, gram_done, sq_done = sem("tr_done"), sem("tr_out"), sem("gram_done"), sem("sq_done")
        v_out = [sem("v_out0"), sem("v_out1")]
        fin, root_done, rn_out = sem("fin"), sem("root_done"), sem("rn_out")
        block = ctx.enter_context(nc.Block())
        src = x3.rearrange("(b p) n -> p b n", p=P)
        vdst = v_dram.rearrange("(b p) n -> p b n", p=P)

        LAST = UNITS + 1

        PEEL = 4

        def rows_of(t):
            return 1 if at(t, UNITS) else PR

        def run(eng, step, tail=STEPS):
            for t in range(PEEL):
                step(t, t % 2)
            with eng.Fori(PEEL // 2, tail // 2) as i:
                step(i * 2, 0, True)
                step(i * 2 + 1, 1, True)
            for t in range(tail, LAST + 1):
                step(t, t % 2)

        @block.sync
        def _(sp):
            for t in range(2):
                sp.dma_start(xf[:, t], src[:, :, t * CHUNK:(t + 1) * CHUNK]).then_inc(x_in[t], 16)
            sp.dma_start(bq[:, :], b_qkv.rearrange("(b p) -> p b", p=P), allow_slow_non_contiguous=True).then_inc(c_in, 16)
            sp.dma_start(bd[:, :], b_dw.rearrange("(b p) -> p b", p=P), allow_slow_non_contiguous=True).then_inc(c_in, 16)
            sp.dma_start(wd[:, :, :], w_dw.rearrange("(b p) o y x -> p b (o y x)", p=P)).then_inc(c_in, 16)

            def step(t, par, inner=False):
                if inner or t + 2 < STEPS:
                    address(sp, (t + 2) * CHUNK)
                    sp.wait_ge(lo_ready, t + 1)
                    sp.dma_start(xf[:, par], src[:, :, bass.ds((t + 2) * CHUNK, CHUNK)]).then_inc(x_in[par], 16)
                if inner or 0 <= t - 1 < UNITS:
                    address(sp, (t - 1) * PX)
                    sp.wait_ge(dw_done, t)
                    n = rows_of(t) * PW
                    sp.dma_start(vdst[:, :, bass.ds((t - 1) * PX, n)], dw[:, 1 - par, QK:QO, 0:n]).then_inc(v_out[1 - par], 16)

            run(sp, step, STEPS - 2)
            sp.wait_ge(fin, 4)
            sp.dma_start(rq_dram.rearrange("(b p) -> p b", p=P), tot[:, 2, :],
                         allow_slow_non_contiguous=True).then_inc(rn_out, 16)
            sp.wait_ge(rn_out, 16)
            sp.wait_ge(v_out[0], 16 * (UNITS // 2 + 1))
            sp.wait_ge(v_out[1], 16 * (UNITS // 2))

        @block.scalar
        def _(act):
            act.wait_ge(prep, 2)
            act.wait_ge(c_in, 48)

            def split(t, par, first=False):
                act.wait_ge(x_in[par], (t // 2) * 16 + 16 if isinstance(t, int) else (t - par) * 8 + 16)
                for b in range(CB):
                    nc.scalar.activation(xf[:, par, b], xf[:, par, b], ACT.Identity,
                                         bias=bx[:, b:b + 1], scale=sx[:, b:b + 1]).then_inc(norm_ready, 1)
                act.wait_ge(norm_ready, t * CB + CB)
                if not first:
                    act.wait_ge(qkv_done, t * GPS - GPS)
                nc.scalar.activation(xhi[:, par], xf[:, par], ACT.Copy).then_inc(hi_ready, 1)

            split(0, 0, True)

            def bands(ix):
                for b in range(CB):
                    if not at(ix, 0):
                        act.wait_ge(band_out[b], ix * 16)
                    for part in range(2):
                        window = bass.AP(padw, (b * 2 + part) * JR * JX + ix,
                                         [[CB * 2 * JR * JX, P], [TW, NU], [JX, JR], [1, TW]])
                        nc.scalar.activation(band[:, b, :, :, :, part].rearrange("p j x u -> p u j x"), window,
                                             ACT.Copy).then_inc(band_made, 1)
                for b in range(CB):
                    act.wait_ge(band_made, ix * (2 * CB) + 2 * b + 2)
                    act.dma_start(toep_dram[b * P:(b + 1) * P, bass.ds(ix, 1), :].rearrange("p a n -> p (a n)"),
                                  band[:, b].rearrange("p j x u a -> p (j x u a)")).then_inc(band_out[b], 16)

            def step(t, par, inner=False):
                u, up = t - 1, 1 - par
                if inner or 0 <= u < UNITS:
                    real = inner or u < STEPS
                    if real:
                        act.wait_ge(max_done, u * GPS + GPS)
                        if inner or u >= 1:
                            act.wait_ge(dw_done, u)
                    else:
                        act.wait_ge(below_zero, 1)
                    act.wait_ge(zeroed, 2)
                    if inner or u >= 2:
                        act.wait_ge(v_out[up], (u - up) * 8)
                        act.wait_ge(tr_done, u * NT - NT)
                        act.wait_ge(sq_done, u * QK - QK)
                    if real:
                        for o in range(QO):
                            nc.scalar.activation(pool[:, up, o, 2:2 + PR, 1:1 + PW], pool[:, up, o, 2:2 + PR, 1:1 + PW],
                                                 ACT.Identity, bias=bq[:, o:o + 1], scale=UNSCALE).then_inc(bias_done, 1)
                    for o in range(QO):
                        if real:
                            act.wait_ge(bias_done, u * QO + o + 1)
                        if inner or u >= 1:
                            act.wait_ge(halo_done, u * QO - QO + o + 1)
                        nc.scalar.activation(dw[:, up, o, :].rearrange("p (y x) -> p y x", y=PR)[:, 0:rows_of(t)],
                                             pool[:, up, o, 0:rows_of(t), 0:PW],
                                             ACT.Identity, bias=bd[:, o:o + 1], scale=wd[:, o, 0:1]).then_inc(tap0_done, 1)
                    if real:
                        for o in range(QO):
                            nc.scalar.activation(pool[:, par, o, 0:2, 1:1 + PW], pool[:, up, o, PR:PR + 2, 1:1 + PW],
                                                 ACT.Copy).then_inc(halo_done, 1)
                u = t - 2
                if inner or 0 <= u < UNITS:
                    if inner or u >= 1:
                        act.wait_ge(gram_done, u)
                    for n in range(2 if at(u, UNITS - 1) else NT):
                        act.wait_ge(tr_done, u * NT + n + 1)
                        nc.scalar.activation(pixT[:, n // 2, n % 2, :], tbank[n % NTB][:, 0:C], ACT.Copy).then_inc(tr_out, 1)
                    act.wait_ge(dw_done, u + 1)
                    for o in range(QK):
                        if inner or u >= 1 or o >= 1:
                            act.wait_ge(sq_done, u * QK + o)
                        n = PW if at(u, UNITS - 1) else PX
                        nc.scalar.activation(sq[:, 0:n], dw[:, par, o, 0:n], ACT.Square,
                                             accum_out=nrm[:, o, bass.ds(u, 1)]).then_inc(sq_done, 1)
                if at(t, 0):
                    split(1, 1, True)
                elif inner or t + 1 < STEPS:
                    split(t + 1, 1 - par)
                if inner or 2 <= t < 2 + TW:
                    if at(t, 2):
                        act.wait_ge(pad_made, 1 + 2 * CB)
                    bands(t - 2)

            run(act, step, 2 + TW)
            for b in range(CB):
                act.wait_ge(band_out[b], 16 * TW)
            act.wait_ge(fin, 1)
            nc.scalar.activation(tot[:, 1, :], tot[:, 0, :], ACT.Sqrt).then_inc(root_done, 1)

        @block.gpsimd
        def _(gp):
            def low(t, par, first=False):
                gp.wait_ge(hi_ready, t + 1)
                if not first:
                    gp.wait_ge(qkv_done, t * GPS - GPS)
                nc.gpsimd.tensor_tensor(xlo[:, par], xf[:, par], xhi[:, par], ALU.subtract).then_inc(lo_ready, 1)

            G = nc.gpsimd
            G.memset(padw[:, :, :, :, :], 0.0).then_inc(pad_made, 1)
            gp.wait_ge(pad_made, 1)
            low(0, 0, True)
            low(1, 1, True)
            for b in range(CB):
                inside = [padw[:, b, k, TH - 1:TH - 1 + KL, TW - 1:TW - 1 + KL] for k in range(2)]
                G.tensor_copy(inside[0], kern[:, b]).then_inc(pad_made, 1)
                gp.wait_ge(pad_made, 2 + 2 * b)
                G.tensor_tensor(inside[1], kern[:, b], inside[0], ALU.subtract).then_inc(pad_made, 1)
            with gp.Fori(1, STEPS // 2) as i:
                low(i * 2, 0)
                low(i * 2 + 1, 1)

        @block.vector
        def _(dve):
            nc.vector.tensor_scalar(sx[:, :], rstd[:, :], SCALE, None, ALU.mult).then_inc(prep, 1)
            dve.wait_ge(prep, 1)
            nc.vector.scalar_tensor_tensor(bx[:, :], mean[:, :], -1.0, sx[:, :], ALU.mult, ALU.mult).then_inc(prep, 1)
            nc.vector.memset(pool[:, :, :, :, 0:PW + 2:PW + 1], 0.0).then_inc(zeroed, 1)
            nc.vector.memset(pool[:, 0, :, 0:2, 1:1 + PW], 0.0).then_inc(zeroed, 1)
            dve.wait_ge(zeroed, 2)
            taps = [(o, k) for k in range(1, TAPS) for o in range(QO)]
            LEAD = 4

            def step(t, par, inner=False):
                u, up = t - 1, 1 - par
                convolve = inner or 0 <= u < UNITS
                done = 0
                for g in range(GPS):
                    if inner or t < STEPS:
                        dve.wait_ge(qkv_done, t * GPS + g + 1)
                        if g == 0 and (inner or t >= 2):
                            dve.wait_ge(halo_done, (t - 1) * QO)
                        j, o = g // QO, g % QO
                        nc.vector.tensor_reduce(
                            pool[:, par, o, 2 + j, 1:1 + PW],
                            qbank[g % NQB][:, 0:2 * W].rearrange("p (r x c) -> p x r c", r=2, c=2),
                            AX.XY, ALU.max).then_inc(max_done, 1)
                    if convolve:
                        upto = max(0, (g + 1 - LEAD)) * len(taps) // (GPS - LEAD)
                        for n in range(done, upto):
                            o, k = taps[n]
                            if k == 1:
                                dve.wait_ge(tap0_done, u * QO + o + 1)
                            else:
                                dve.wait_ge(taps_done, u * len(taps) + n - QO + 1)
                            y, x = k // KS, k % KS
                            acc = dw[:, up, o, :].rearrange("p (y x) -> p y x", y=PR)[:, 0:rows_of(t)]
                            nc.vector.scalar_tensor_tensor(acc, pool[:, up, o, y:y + rows_of(t), x:x + PW], wd[:, o, k:k + 1], acc,
                                                           ALU.mult, ALU.add).then_inc(taps_done, 1)
                        done = upto
                if convolve:
                    dve.wait_ge(taps_done, u * len(taps) + len(taps))
                    if at(t, 1):
                        nc.vector.memset(dw[:, up, 0:QK, 0:PW], 0.0).then_inc(dw_done, 1)
                    elif at(t, UNITS):
                        nc.vector.memset(dw[:, up, 0:QK, PW:P], 0.0).then_inc(dw_done, 1)
                    else:
                        dve.sem_inc(dw_done, 1)
                if at(t, STEPS - 1):
                    nc.vector.memset(pool[:, 0, :, 2:2 + PR, 1:1 + PW], 0.0).then_inc(below_zero, 1)

            run(dve, step, STEPS - 2)
            dve.wait_ge(sq_done, UNITS * QK)
            nc.vector.tensor_reduce(tot[:, 0, :], nrm[:, :, :], AX.X, ALU.add).then_inc(fin, 1)
            dve.wait_ge(root_done, 1)
            nc.vector.tensor_scalar(tot[:, 1, :], tot[:, 1, :], 1e-12, None, ALU.max).then_inc(fin, 1)
            dve.wait_ge(fin, 2)
            nc.vector.reciprocal(tot[:, 2, :], tot[:, 1, :]).then_inc(fin, 2)

        @block.tensor
        def _(pe):
            TR_AT = {10: range(0, 3), 12: range(3, 6)}
            GRAM_AT = 16

            def transposes(u, par, ns, inner):
                if ns[0] == 0:
                    pe.wait_ge(dw_done, u + 1)
                for n in ns:
                    if inner or u >= 1 or n >= NTB:
                        pe.wait_ge(tr_out, u * NT + n - NTB + 1)
                    px, qk = n // 2, n % 2
                    for b in range(CB):
                        ins = nc.tensor.transpose(tbank[n % NTB][:, b * P:(b + 1) * P],
                                                  dw[:, par, qk * CB + b, px * P:(px + 1) * P], ident[:, :])
                    ins.then_inc(tr_done, 1)

            def grams(u):
                tiles = 1 if at(u, UNITS - 1) else NTP
                pe.wait_ge(tr_out, u * NT + 2 * tiles)
                for px in range(tiles):
                    for h in range(NPAIR):
                        first = at(u, 0) and px == 0 and h == 0
                        last = at(u, UNITS - 1)
                        ins = nc.tensor.matmul(gram[0:PAIR, h * PAIR:(h + 1) * PAIR],
                                               pixT[:, px, 0, h * PAIR:(h + 1) * PAIR],
                                               pixT[:, px, 1, h * PAIR:(h + 1) * PAIR],
                                               start=first, stop=last, skip_group_check=True)
                ins.then_inc(gram_done, 1)

            def step(t, par, inner=False):
                tail = inner or 0 <= t - 2 < UNITS
                if inner or t < STEPS:
                    pe.wait_ge(lo_ready, t + 1)
                for g in range(GPS):
                    if inner or t < STEPS:
                        if inner or t >= 1 or g >= NQB:
                            pe.wait_ge(max_done, t * GPS + g - NQB + 1)
                        j, o = g // QO, g % QO
                        n = 0
                        for b in range(CB):
                            for w, x in ((whi, xhi), (whi, xlo), (wlo, xhi)):
                                ins = nc.tensor.matmul(qbank[g % NQB][:, 0:2 * W], w[:, b, o * P:(o + 1) * P],
                                                       x[:, par, b, j * 2 * W:(j + 1) * 2 * W],
                                                       start=n == 0, stop=n == CB * PASSES - 1)
                                n += 1
                        ins.then_inc(qkv_done, 1)
                    if tail and g in TR_AT:
                        ns = [n for n in TR_AT[g] if n < 2 or not at(t - 2, UNITS - 1)]
                        if ns:
                            transposes(t - 2, par, ns, inner)
                    if tail and g == GRAM_AT:
                        grams(t - 2)

            run(pe, step)


def stage_attention(nc, gram, rq_dram, temp, scales, pt_dram, ident, pt, project):
    with ExitStack() as ctx:
        def sb(name, shape):
            return ctx.enter_context(nc.sbuf_tensor(f"at_{name}", shape, F32))

        def sem(name):
            return ctx.enter_context(nc.semaphore(f"at_{name}"))

        rowq = sb("rowq", [PAIR, NPAIR])
        colk = sb("colk", [PAIR, NPAIR, PAIR])
        tq = sb("tq", [PAIR, NPAIR])
        av = sb("av", [PAIR, len(TOPK)])
        half = sb("half", [PAIR, 2])
        full = sb("full", [PAIR, NPAIR, PAIR])
        lower = sb("lower", [PAIR, NPAIR, HC])
        att = sb("att", [PAIR, NPAIR, HC])
        left = sb("left", [PAIR, len(TOPK), NPAIR, HC])
        top = sb("top", [PAIR, NPAIR, 5, 8])
        nmax = sb("nmax", [PAIR, NPAIR])
        ex = sb("ex", [PAIR, NPAIR, HC])
        kept = sb("kept", [PAIR, len(TOPK), NPAIR, HC])
        total = sb("total", [PAIR, len(TOPK), NPAIR])
        coef = sb("coef", [PAIR, len(TOPK), NPAIR])
        prob = sb("prob", [PAIR, NPAIR, HC])
        wide = sb("wide", [PAIR, NPAIR, PAIR])
        zero = sb("zero", [P, CB, C])
        ptT = sb("ptT", [PAIR, NPAIR, PAIR])
        tps = ctx.enter_context(nc.psum_tensor("at_tps", [P, 512], F32))
        c_in, link, halves, nmax_ready, exp_done, turned, zero_ready, out_done = (
            sem("c_in"), sem("link"), sem("halves"), sem("nmax_ready"), sem("exp_done"), sem("turned"),
            sem("zero_ready"), sem("out_done"))
        wide_ready, ptT_ready, pt_in = sem("wide_ready"), sem("ptT_ready"), sem("pt_in")
        block = ctx.enter_context(nc.Block())

        @block.sync
        def _(sp):
            sp.dma_start(rowq[:, :], rq_dram[0:C].rearrange("(h p) -> p h", p=PAIR),
                         allow_slow_non_contiguous=True).then_inc(c_in, 16)
            sp.dma_start(colk[:, :, :].rearrange("p h n -> p (h n)"),
                         rq_dram[C:2 * C].unsqueeze(0).broadcast_to([PAIR, C])).then_inc(c_in, 16)
            t2 = temp.rearrange("(h two) a b -> two (h a b)", two=2)
            for s in range(2):
                sp.dma_start(tq[s * HC:(s + 1) * HC, :], t2[s:s + 1, :].broadcast_to([HC, NPAIR]),
                             allow_slow_non_contiguous=True).then_inc(c_in, 16)
            for n, a in enumerate(scales):
                sp.dma_start(av[:, n:n + 1], a.unsqueeze(0).broadcast_to([PAIR, 1]),
                             allow_slow_non_contiguous=True).then_inc(c_in, 16)
            sp.wait_ge(zero_ready, 1)
            sp.dma_start(pt_dram.rearrange("(b p) n -> p b n", p=P), zero[:, :, :]).then_inc(out_done, 16)
            project.first_loads(sp)
            sp.wait_ge(out_done, 16)
            sp.wait_ge(ptT_ready, 1)
            for h in range(NPAIR):
                sp.dma_start(pt_dram[h * PAIR:(h + 1) * PAIR, h * PAIR:(h + 1) * PAIR], ptT[:, h, :]).then_inc(out_done, 16)
            sp.wait_ge(out_done, 16 + 16 * NPAIR)
            sp.dma_start(pt[:, :, :], pt_dram.rearrange("(b p) n -> p b n", p=P)).then_inc(pt_in, 16)
            sp.wait_ge(pt_in, 16)

        @block.gpsimd
        def _(gp):
            nc.gpsimd.memset(half[:, :], 1.0).then_inc(halves, 1)
            gp.wait_ge(halves, 1)
            nc.gpsimd.affine_select(half[:, 0:1], half[:, 0:1], [[0, 1]], ALU.is_ge, 0.0,
                                    base=HC - 1, channel_multiplier=-1).then_inc(halves, 1)
            nc.gpsimd.affine_select(half[:, 1:2], half[:, 1:2], [[0, 1]], ALU.is_ge, 0.0,
                                    base=-HC, channel_multiplier=1).then_inc(halves, 1)
            nc.gpsimd.memset(zero[:, :, :], 0.0).then_inc(zero_ready, 1)
            project.padding(gp)

        @block.scalar
        def _(act):
            act.wait_ge(nmax_ready, 1)
            for h in range(NPAIR):
                nc.scalar.activation(ex[:, h, :], att[:, h, :], ACT.Exp, bias=nmax[:, h:h + 1]).then_inc(exp_done, 1)

        @block.vector
        def _(dve):
            count = [0]

            def chained(ins):
                count[0] += 1
                ins.then_inc(link, 1)
                dve.wait_ge(link, count[0])

            V = nc.vector
            dve.wait_ge(c_in, 16 * (4 + len(scales)))
            dve.wait_ge(halves, 3)
            chained(V.tensor_tensor(full[:, :, :], gram[0:PAIR, 0:C].rearrange("p (h n) -> p h n", h=NPAIR),
                                    colk[:, :, :], ALU.mult))
            for h in range(NPAIR):
                chained(V.tensor_scalar(full[:, h, :], full[:, h, :], rowq[:, h:h + 1], tq[:, h:h + 1], ALU.mult, ALU.mult))
            chained(V.tensor_scalar(lower[:, :, :], full[:, :, HC:PAIR], half[:, 1:2], None, ALU.mult))
            chained(V.scalar_tensor_tensor(att[:, :, :], full[:, :, 0:HC], half[:, 0:1], lower[:, :, :], ALU.mult, ALU.add))
            rounds = TOPK[1] // 8
            for h in range(NPAIR):
                cur = att[:, h, :]
                for r in range(rounds):
                    chained(V.max(top[:, h, r, :], cur))
                    nxt = left[:, 0, h, :] if (r + 1) * 8 <= TOPK[0] else left[:, 1, h, :]
                    chained(V.match_replace(nxt, top[:, h, r, :], cur, TAKEN))
                    cur = nxt
                for k in (3, 2):
                    chained(V.max(top[:, h, rounds, :], left[:, 1, h, :]))
                    chained(V.memset(top[:, h, rounds, TOPK[k] - TOPK[1]:8], TAKEN))
                    chained(V.match_replace(left[:, k, h, :], top[:, h, rounds, :], left[:, 1, h, :], TAKEN))
            V.tensor_scalar(nmax[:, :], top[:, :, 0, 0], -1.0, None, ALU.mult).then_inc(nmax_ready, 1)
            dve.wait_ge(exp_done, NPAIR)
            for k in range(len(TOPK)):
                chained(V.scalar_tensor_tensor(kept[:, k], left[:, k], TAKEN, ex[:, :, :], ALU.is_equal, ALU.mult))
            chained(V.tensor_reduce(total[:, :, :], kept[:, :, :, :], AX.X, ALU.add))
            chained(V.reciprocal(coef[:, :, :], total[:, :, :]))
            for k in range(len(TOPK)):
                chained(V.tensor_scalar(coef[:, k, :], coef[:, k, :], av[:, k:k + 1], None, ALU.mult))
            for k in range(len(TOPK)):
                chained(V.tensor_tensor(kept[:, k], kept[:, k], coef[:, k].unsqueeze(2).broadcast_to([PAIR, NPAIR, HC]),
                                        ALU.mult))
            chained(V.tensor_reduce(prob[:, :, :], kept[:, :, :, :].rearrange("p k h n -> p h n k"), AX.X, ALU.add))
            V.tensor_scalar(wide[:, :, 0:HC], prob[:, :, :], half[:, 0:1], None, ALU.mult).then_inc(wide_ready, 1)
            V.tensor_scalar(wide[:, :, HC:PAIR], prob[:, :, :], half[:, 1:2], None, ALU.mult).then_inc(wide_ready, 1)
            dve.wait_ge(turned, 1)
            V.tensor_copy(ptT[:, :, :], tps[0:PAIR, 0:C].rearrange("p (h n) -> p h n", h=NPAIR)).then_inc(ptT_ready, 1)

        @block.tensor
        def _(pe):
            pe.wait_ge(wide_ready, 2)
            for h in range(NPAIR):
                ins = nc.tensor.transpose(tps[0:PAIR, h * PAIR:(h + 1) * PAIR], wide[:, h, :], ident[0:PAIR, 0:PAIR])
            ins.then_inc(turned, 1)


def project_start(nc, ctx, x3, v_dram, wpT, b_proj):
    def sb(name, shape, dt=F32):
        return ctx.enter_context(nc.sbuf_tensor(f"pr_{name}", shape, dt))

    def sem(name):
        return ctx.enter_context(nc.semaphore(f"pr_{name}"))

    vb = sb("vb", [P, 2, CB, PX])
    xb = sb("xb", [P, 2, CB, CHUNK])
    x1 = sb("x1", [P, 2, CB, TJ, TW, TH])
    wp = sb("wp", [P, CB, C])
    bp = sb("bp", [P, CB])
    c_in, zeroed = sem("c_in"), sem("zeroed")
    v_in = [sem("v_in0"), sem("v_in1")]
    x_in = [sem("x_in0"), sem("x_in1")]
    src = x3.rearrange("(b p) n -> p b n", p=P)
    vsrc = v_dram.rearrange("(b p) n -> p b n", p=P)

    def load(sp, t, par):
        sp.dma_start(vb[:, par], vsrc[:, :, bass.ds(t * PX + PW, PX)]).then_inc(v_in[par], 16)
        sp.dma_start(xb[:, par], src[:, :, bass.ds(t * CHUNK, CHUNK)]).then_inc(x_in[par], 16)

    def first_loads(sp):
        sp.dma_start(wp[:, :, :], wpT.rearrange("(b p) n -> p b n", p=P)).then_inc(c_in, 16)
        sp.dma_start(bp[:, :], b_proj.rearrange("(b p) -> p b", p=P), allow_slow_non_contiguous=True).then_inc(c_in, 16)
        load(sp, 0, 0)
        load(sp, 1, 1)

    def padding(gp):
        flat = x1[:, :, :, :, :, :].rearrange("p r b j x y -> p (r b) (j x y)")
        nc.gpsimd.memset(flat[:, :, 0:PAD * TH], 0.0).then_inc(zeroed, 1)
        nc.gpsimd.memset(flat[:, :, (PAD + W) * TH:XW * TH], 0.0).then_inc(zeroed, 1)
        nc.gpsimd.memset(flat[:, 0:CB, PAD * TH:(PAD + W) * TH].rearrange("p b (x y) -> p b x y", y=TH)[:, :, :, 0:PAD],
                         0.0).then_inc(zeroed, 1)

    start = Shared()
    start.vb, start.xb, start.x1, start.wp, start.bp = vb, xb, x1, wp, bp
    start.c_in, start.zeroed, start.v_in, start.x_in = c_in, zeroed, v_in, x_in
    start.load, start.first_loads, start.padding = load, first_loads, padding
    return start


def stage_project(nc, start, pt, ident, stats, patch_dram):
    NTR = 4
    runs = [(b, j, min(NTR, TJ - j)) for b in range(CB) for j in range(0, TJ, NTR)]
    NRUN = len(runs)
    RPB = NRUN // CB
    FIRST_REC, REC = 1, 3
    need = [sorted({c // P for h in range(HEADS) if h * HC < (o + 1) * P and (h + 1) * HC > o * P
                    for c in (h * HC, (h + 1) * HC - 1)}) for o in range(CB)]
    with ExitStack() as ctx:
        def sb(name, shape, dt=F32):
            return ctx.enter_context(nc.sbuf_tensor(f"pr_{name}", shape, dt))

        def sem(name):
            return ctx.enter_context(nc.semaphore(f"pr_{name}"))

        vb, xb, x1, wp, bp, c_in, zeroed = start.vb, start.xb, start.x1, start.wp, start.bp, start.c_in, start.zeroed
        v_in, x_in = start.v_in, start.x_in
        ge = sb("ge", [P, CB, PX])
        turned = sb("turned", [P, CB, P, TJ])
        abank = [ctx.enter_context(nc.psum_tensor(f"pr_ab{i}", [P, 512], F32)) for i in range(CB)]
        ybank = [ctx.enter_context(nc.psum_tensor(f"pr_yb{i}", [P, 512], F32)) for i in range(CB)]
        tbank = [ctx.enter_context(nc.psum_tensor(f"pr_tb{i}", [P, 512], F32)) for i in range(2)]
        att_done, gelu_done, proj_done, y_ready = sem("att_done"), sem("gelu_done"), sem("proj_done"), sem("y_ready")
        x1_done, st_done = sem("x1_done"), sem("st_done")
        tr_done, tr_out = sem("tr_done"), sem("tr_out")
        stored = [sem(f"stored{b}") for b in range(CB)]
        block = ctx.enter_context(nc.Block())

        def run(eng, step, head=2, tail=STEPS):
            for t in range(head):
                step(t, t % 2)
            with eng.Fori(head // 2, tail // 2) as i:
                step(i * 2, 0, True)
                step(i * 2 + 1, 1, True)
            for t in range(tail, STEPS + 1):
                step(t, t % 2)

        @block.sync
        def _(sp):
            def step(t, par, inner=False):
                if inner or t >= 1:
                    for b in range(CB):
                        address(sp, (t - 1) * (GRP * TJ) + b * (P // GRP) * TI * GRP * TJ)
                        sp.wait_ge(tr_out, t * NRUN - NRUN + (b + 1) * RPB)
                        sp.dma_start(
                            patch_dram[:, b * (P // GRP):(b + 1) * (P // GRP), bass.ds(t - 1, 1), :].rearrange("p g a n -> p g (a n)"),
                            turned[:, b].rearrange("p (g c) j -> p g (c j)", c=GRP)).then_inc(stored[b], 16)
                if inner or t + 2 < STEPS:
                    address(sp, (t + 2) * PX + PW)
                    address(sp, (t + 2) * CHUNK)
                    if inner:
                        sp.compute_val(t * CB + CB)
                    sp.wait_ge(att_done, t * CB + CB)
                    sp.wait_ge(x1_done, t * CB + CB)
                    start.load(sp, t + 2, par)

            run(sp, step, tail=STEPS - 2)
            for b in range(CB):
                sp.wait_ge(tr_out, STEPS * NRUN + (b + 1) * RPB)
                sp.dma_start(patch_dram[:, b * (P // GRP):(b + 1) * (P // GRP), STEPS, :],
                             turned[:, b].rearrange("p (g c) j -> p g (c j)", c=GRP)).then_inc(stored[b], 16)
            for b in range(CB):
                sp.wait_ge(stored[b], 16 * (STEPS + 1))

        ORDER = ("A0", "A1", "T0", "T1", "A2", "T2", "T3", "T4", "Y0", "T5", "T6", "Y1", "T7", "T8", "Y2", "T9", "T10", "T11")

        @block.scalar
        def _(act):
            def evacuate(t, n):
                b, j, k = runs[n]
                if n % RPB == 0 and not at(t, 0):
                    act.wait_ge(stored[b], t * 16)
                act.wait_ge(tr_done, t * NRUN + n + 1)
                nc.scalar.activation(turned[:, b, :, j:j + k].rearrange("p c j -> p j c"),
                                     tbank[n % 2][:, 0:k * P].rearrange("p (j c) -> p j c", j=k),
                                     ACT.Copy).then_inc(tr_out, 1)

            def step(t, par, inner=False):
                for kind, n in ((w[0], int(w[1:])) for w in ORDER):
                    if kind == "T" and (inner or t >= 1):
                        evacuate(t - 1, n)
                    elif kind == "A" and (inner or t < STEPS):
                        if n == 0 and (inner or t >= 1):
                            act.wait_ge(proj_done, t * CB)
                        act.wait_ge(att_done, t * CB + n + 1)
                        nc.scalar.activation(ge[:, n, :], abank[n][:, 0:PX], ACT.Gelu).then_inc(gelu_done, 1)
                    elif kind == "Y" and (inner or t < STEPS):
                        act.wait_ge(proj_done, t * CB + n + 1)
                        nc.scalar.activation(ybank[n][:, 0:PX], ybank[n][:, 0:PX], ACT.Identity,
                                             bias=bp[:, n:n + 1]).then_inc(y_ready, 1)

            act.wait_ge(c_in, 32)
            run(act, step)
            for n in range(NRUN):
                evacuate(STEPS, n)

        @block.vector
        def _(dve):
            dve.wait_ge(zeroed, 3)

            def add(par, b, buf, y, row, n):
                out = x1[:, buf, b].rearrange("p j x y -> p (j x) y")[:, PAD:PAD + W, row:row + 2 * n - 1:2]
                x = xb[:, par, b, :].rearrange("p (y x c) -> p y x c", x=PW, c=2)[:, y:y + 2 * n - 1:2]
                low = ybank[b][:, y // 2 * PW:(y // 2 + n) * PW].rearrange("p (y x) -> p y x", y=n)
                return nc.vector.tensor_tensor(out.rearrange("p (x c) y -> p y x c", c=2), x,
                                               low.unsqueeze(3).broadcast_to([P, n, PW, 2]), ALU.add)

            def record(n, b, pixels):
                return nc.vector.bn_stats(stats[:, b, bass.ds(n, 1), :].rearrange("p a s -> p (a s)"), pixels)

            def step(t, par, inner=False):
                if inner or t < STEPS:
                    dve.wait_ge(x_in[par], (t // 2) * 16 + 16 if isinstance(t, int) else (t - par) * 8 + 16)
                    for b in range(CB):
                        if inner or t >= 1:
                            dve.wait_ge(tr_done, t * NRUN - NRUN + (b + 1) * RPB)
                            dve.wait_ge(st_done, t * CB - CB + b + 1)
                        dve.wait_ge(y_ready, t * CB + b + 1)
                        for r in range(2):
                            add(par, b, par, r, PAD + r, 1)
                            ins = add(par, b, 1 - par, 2 + r, r, PAD // 2)
                        ins.then_inc(x1_done, 1)
                        dve.wait_ge(x1_done, t * CB + b + 1)
                        flat = x1[:, par, b].rearrange("p j x y -> p (j x) y")[:, PAD:PAD + W, :]
                        if at(t, 0):
                            ins = record(0, b, flat[:, :, PAD:TH])
                        else:
                            for k in range(REC):
                                ins = record(t * REC - REC + FIRST_REC + k, b,
                                             flat[:, k * W // REC:(k + 1) * W // REC, :].rearrange("p x y -> p (x y)"))
                        ins.then_inc(st_done, 1)

            run(dve, step)
            for b in range(CB):
                flat = x1[:, STEPS % 2, b].rearrange("p j x y -> p (j x) y")[:, PAD:PAD + W, :]
                for k in range(REC):
                    ins = record(STEPS * REC - REC + FIRST_REC + k, b, flat[:, k * W // REC:(k + 1) * W // REC, 0:PAD])
            ins.then_inc(st_done, 1)
            dve.wait_ge(st_done, STEPS * CB + 1)

        @block.tensor
        def _(pe):
            pe.wait_ge(c_in, 32)

            def patches(t, par, n):
                b, j0, k = runs[n]
                if n % RPB == 0:
                    pe.wait_ge(x1_done, STEPS * CB if at(t, STEPS) else t * CB + b + 1)
                if not (at(t, 0) and n < 2):
                    pe.wait_ge(tr_out, t * NRUN + n - 1)
                for j in range(k):
                    ins = nc.tensor.transpose(tbank[n % 2][:, j * P:(j + 1) * P],
                                              x1[:, par, b, j0 + j].rearrange("p x y -> p (x y)"), ident[:, :])
                ins.then_inc(tr_done, 1)

            def step(t, par, inner=False):
                for kind, n in ((w[0], int(w[1:])) for w in ORDER):
                    if kind == "T" and (inner or t >= 1):
                        patches(t - 1, 1 - par, n)
                    elif kind == "A" and (inner or t < STEPS):
                        if n == 0:
                            pe.wait_ge(v_in[par], (t // 2) * 16 + 16 if isinstance(t, int) else (t - par) * 8 + 16)
                        if inner or t >= 1:
                            pe.wait_ge(gelu_done, t * CB - CB + n + 1)
                        for k, b in enumerate(need[n]):
                            ins = nc.tensor.matmul(abank[n][:, 0:PX], pt[:, b, n * P:(n + 1) * P], vb[:, par, b, :],
                                                   start=k == 0, stop=k == len(need[n]) - 1)
                        ins.then_inc(att_done, 1)
                    elif kind == "Y" and (inner or t < STEPS):
                        if n == 0:
                            pe.wait_ge(gelu_done, t * CB + CB)
                        if inner or t >= 1:
                            pe.wait_ge(x1_done, t * CB - CB + n + 1)
                        for b in range(CB):
                            ins = nc.tensor.matmul(ybank[n][:, 0:PX], wp[:, b, n * P:(n + 1) * P], ge[:, b, :],
                                                   start=b == 0, stop=b == CB - 1)
                        ins.then_inc(proj_done, 1)

            run(pe, step)
            for n in range(NRUN):
                patches(STEPS, STEPS % 2, n)


def stage_kernels(nc, kern, scale, shift, mean, rstd, toep_dram, const_dram):
    with ExitStack() as ctx:
        def sb(name, shape, dt=F32):
            return ctx.enter_context(nc.sbuf_tensor(f"kn_{name}", shape, dt))

        def sem(name):
            return ctx.enter_context(nc.semaphore(f"kn_{name}"))

        mid = KL // 2
        inv = sb("inv", [P, CB])
        cst = sb("cst", [P, CB, 3])
        padr = sb("padr", [P, CB, 2, JX], F16)
        row = sb("row", [P, CB, TW, TW, NU, 2], F16)
        link, pad_zero, pad_ready, made, sent, cst_ready, cst_out = (
            sem("link"), sem("pad_zero"), sem("pad_ready"), sem("made"), sem("sent"), sem("cst_ready"), sem("cst_out"))
        block = ctx.enter_context(nc.Block())
        RUN = TW * NU * 2
        jobs = [(b, part, u) for b in range(CB) for part in range(2) for u in range(NU)]

        def make(eng, who, copy):
            eng.wait_ge(pad_ready, 1)
            for n, (b, part, u) in enumerate(jobs):
                if n % 3 == who:
                    window = bass.AP(padr, (b * 2 + part) * JX + u * TW, [[CB * 2 * JX, P], [1, TW], [1, TW]])
                    copy(row[:, b, :, :, u, part], window).then_inc(made, 1)

        @block.sync
        def _(sp):
            sp.wait_ge(made, len(jobs))
            for b in range(CB):
                sp.dma_start(toep_dram[b * P:(b + 1) * P, :, (TH - 1 + mid) * RUN:(TH + mid) * RUN],
                             row[:, b].rearrange("p i x u a -> p i (x u a)")).then_inc(sent, 16)
            sp.wait_ge(cst_ready, 1)
            sp.dma_start(const_dram.rearrange("(b p) s -> p b s", p=P), cst[:, :, :],
                         allow_slow_non_contiguous=True).then_inc(cst_out, 16)
            sp.wait_ge(sent, 16 * CB)
            sp.wait_ge(cst_out, 16)

        @block.scalar
        def _(act):
            make(act, 1, lambda o, i: nc.scalar.activation(o, i, ACT.Copy))

        @block.gpsimd
        def _(gp):
            nc.gpsimd.memset(padr[:, :, :, :], 0.0).then_inc(pad_zero, 1)
            make(gp, 2, nc.gpsimd.tensor_copy)

        @block.vector
        def _(dve):
            V = nc.vector
            count = [0]

            def chained(ins):
                count[0] += 1
                ins.then_inc(link, 1)
                dve.wait_ge(link, count[0])

            chained(V.reciprocal(inv[:, :], rstd[:, :]))
            chained(V.tensor_tensor(inv[:, :], inv[:, :], scale[:, 2, :], ALU.add))
            centre = kern[:, :, mid, mid]
            chained(V.scalar_tensor_tensor(centre, inv[:, :], SCALE, centre, ALU.mult, ALU.add))
            dve.wait_ge(pad_zero, 1)
            parts = [padr[:, :, k, TW - 1:TW - 1 + KL] for k in range(2)]
            chained(V.tensor_copy(parts[0], kern[:, :, mid, :]))
            V.tensor_tensor(parts[1], kern[:, :, mid, :], parts[0], ALU.subtract).then_inc(pad_ready, 1)
            make(dve, 0, V.tensor_copy)
            chained(V.tensor_copy(cst[:, :, 0], mean[:, :]))
            chained(V.tensor_scalar(cst[:, :, 1], rstd[:, :], SCALE, None, ALU.mult))
            chained(V.tensor_tensor(cst[:, :, 2], mean[:, :], shift[:, 0, :], ALU.add))
            chained(V.tensor_tensor(cst[:, :, 2], cst[:, :, 2], shift[:, 1, :], ALU.add))
            V.tensor_tensor(cst[:, :, 2], cst[:, :, 2], shift[:, 2, :], ALU.add).then_inc(cst_ready, 1)


def depthwise_start(nc, ctx, patch_dram):
    def sb(name, shape):
        return ctx.enter_context(nc.sbuf_tensor(f"cv_{name}", shape, F32))

    raw = sb("raw", [P, 2, TI, GRP, TJ])
    side = sb("side", [P, 4])
    rowsel = sb("rowsel", [P, TW])
    raw_in = [ctx.enter_context(nc.semaphore(f"cv_raw_in{i}")) for i in range(2)]
    masked = ctx.enter_context(nc.semaphore("cv_masked"))

    def load_group(sp, g, par):
        sp.dma_start(raw[:, par].rearrange("p i c j -> p (i c j)"),
                     patch_dram[:, bass.ds(g, 1), :, :].rearrange("p a i n -> p (a i n)")).then_inc(raw_in[par], 16)

    def first_load(sp):
        load_group(sp, 0, 0)

    def masks(gp):
        nc.gpsimd.memset(side[:, :], 1.0).then_inc(masked, 1)
        gp.wait_ge(masked, 1)
        nc.gpsimd.affine_select(side[:, 0:1], side[:, 0:1], [[0, 1]], ALU.is_ge, 0.0,
                                base=-PAD * TH, channel_multiplier=1).then_inc(masked, 1)
        nc.gpsimd.affine_select(side[:, 1:2], side[:, 1:2], [[0, 1]], ALU.is_ge, 0.0,
                                base=PAD * TH - 1, channel_multiplier=-1).then_inc(masked, 1)
        nc.gpsimd.memset(rowsel[:, :], 1.0).then_inc(masked, 1)
        gp.wait_ge(masked, 4)
        nc.gpsimd.affine_select(rowsel[:, :], rowsel[:, :], [[-TH, TW]], ALU.is_ge, 0.0,
                                base=-PAD, channel_multiplier=1).then_inc(masked, 1)
        gp.wait_ge(masked, 5)
        nc.gpsimd.affine_select(rowsel[:, :], rowsel[:, :], [[TH, TW]], ALU.is_ge, 0.0,
                                base=TH - 1, channel_multiplier=-1).then_inc(masked, 1)

    start = Shared()
    start.raw, start.side, start.rowsel, start.raw_in, start.masked = raw, side, rowsel, raw_in, masked
    start.load_group, start.first_load, start.masks = load_group, first_load, masks
    return start


def stage_depthwise(nc, start, toep_dram, const_dram, ident, out3):
    NTOEP = 8
    NCB = 4
    NBB = 3
    TPB = 4
    FILLS = NBAND * OJ // TPB
    NPIX = OI * OJ
    with ExitStack() as ctx:
        def sb(name, shape, dt=F32):
            return ctx.enter_context(nc.sbuf_tensor(f"cv_{name}", shape, dt))

        def sem(name):
            return ctx.enter_context(nc.semaphore(f"cv_{name}"))

        raw, side, rowsel, raw_in, masked = start.raw, start.side, start.rowsel, start.raw_in, start.masked
        hi = sb("hi", [P, 2, TI, GRP, TJ], F16)
        lo = sb("lo", [P, 2, TI, GRP, TJ], F16)
        cst = sb("cst", [P, C, 3])
        toep = sb("toep", [P, NTOEP, KRUN], F16)
        res = sb("res", [P, 2, NBAND, OJ, GRP, BAND])
        rows = sb("rows", [P, NBAND, TH, W])
        cbank = [ctx.enter_context(nc.psum_tensor(f"cv_cb{i}", [P, 512], F32)) for i in range(NCB)]
        bbank = [ctx.enter_context(nc.psum_tensor(f"cv_bb{i}", [P, 512], F32)) for i in range(NBB)]
        cst_in = sem("cst_in")
        toep_in = [sem(f"toep_in{i}") for i in range(NTOEP)]
        side_ready = sem("side_ready")
        norm_done, edge_done, hi_done, lo_done = (sem("norm_done"), sem("edge_done"),
                                                         sem("hi_done"), sem("lo_done"))
        conv_done, res_done, back_done, rows_done = (sem("conv_done"), sem("res_done"), sem("back_done"),
                                                     sem("rows_done"))
        out_done = [sem(f"out_done{i}") for i in range(NBAND)]
        block = ctx.enter_context(nc.Block())
        shift = [(s, u) for s in range(NS) for u in range(NU)]

        def run(eng, step, tail=NG):
            step(0, 0)
            step(1, 1)
            with eng.Fori(1, tail // 2) as i:
                step(i * 2, 0, True)
                step(i * 2 + 1, 1, True)
            for g in range(tail, NG + 1):
                step(g, g % 2)

        @block.sync
        def _(sp):
            sp.dma_start(cst[:, :, :].rearrange("p c s -> p (c s)"),
                         const_dram.rearrange("c s -> (c s)").unsqueeze(0).broadcast_to([P, C * 3])).then_inc(cst_in, 16)

            def step(g, par, inner=False):
                for c in range(GRP):
                    if at(g, 0) and c == 2:
                        start.load_group(sp, 1, 1)
                    if c == GRP // 2 and (inner or g + 2 < NG):
                        address(sp, (g + 2) * (TI * GRP * TJ))
                        sp.wait_ge(lo_done, g + 1)
                        start.load_group(sp, g + 2, par)
                    if inner or g < NG:
                        address(sp, (g * GRP + c) * (TW * JR * TW * NU * 2), 2)
                        if inner or g * GRP + c >= NTOEP:
                            sp.wait_ge(conv_done, g * GRP + c - NTOEP + 1)
                        sp.dma_start(toep[:, c % NTOEP],
                                     toep_rows(g * GRP + c)).then_inc(toep_in[c % NTOEP], 16)

            def toep_rows(ch):
                v = toep_dram[bass.ds(ch, 1), :, :].rearrange("a i n -> (a i) n")
                return bass.AP(v.tensor, v.offset, [[JR * TW * NU * 2, TW], [TW * NU * 2, TH], [1, KRUN]])

            run(sp, step, tail=NG - 2)

        @block.scalar
        def _(act):
            STORE_AT = (7, 10, 13)

            def store(g, bd):
                act.wait_ge(rows_done, g * FILLS + (bd + 1) * (FILLS // NBAND))
                act.dma_start(out3[bass.ds(g * GRP, GRP), bd * BAND * TH * W:(bd + 1) * BAND * TH * W]
                              .rearrange("c (t n) -> c t n", t=BAND),
                              rows[:, bd].rearrange("p y x -> p (y x)")).then_inc(out_done[bd], 16)

            act.wait_ge(cst_in, 16)

            def split(g, par):
                act.wait_ge(edge_done, g + 1)
                if not (isinstance(g, int) and g < 2):
                    act.wait_ge(conv_done, g * GRP - GRP)
                nc.scalar.activation(hi[:, par], raw[:, par], ACT.Copy).then_inc(hi_done, 1)

            split(0, 0)

            def step(g, par, inner=False):
                if not inner and g >= NG:
                    for bd in range(NBAND):
                        store(g - 1, bd)
                    return
                if inner or g >= 2:
                    act.wait_ge(back_done, g * FILLS - FILLS)
                for c in range(GRP):
                    if (inner or g >= 1) and c in STORE_AT:
                        store(g - 1, STORE_AT.index(c))
                    act.wait_ge(conv_done, g * GRP + c + 1)
                    nc.scalar.activation(res[:, par, :, :, c, :],
                                         cbank[c % NCB][:, 0:NPIX].rearrange("p (b i j) -> p b j i", b=NBAND, j=OJ),
                                         ACT.Identity, bias=cst[:, bass.ds(g * GRP + c, 1), 2], scale=UNSCALE).then_inc(res_done, 1)
                    if c == GRP // 4 and (inner or g + 1 < NG):
                        split(g + 1, 1 - par)

            run(act, step, tail=NG - 2)
            for bd in range(NBAND):
                act.wait_ge(out_done[bd], 16 * NG)

        @block.vector
        def _(dve):
            V = nc.vector
            EDGES = 4
            dve.wait_ge(masked, 6)
            V.tensor_reduce(side[:, 2:3], rowsel[:, :], AX.X, ALU.add).then_inc(side_ready, 1)
            dve.wait_ge(side_ready, 1)
            V.tensor_scalar(side[:, 3:4], side[:, 2:3], -1.0, 1.0, ALU.mult, ALU.add).then_inc(side_ready, 1)
            dve.wait_ge(side_ready, 2)
            dve.wait_ge(cst_in, 16)

            def normalise(g, par):
                dve.wait_ge(raw_in[par], (g // 2) * 16 + 16 if isinstance(g, int) else (g - par) * 8 + 16)
                for c in range(GRP):
                    V.tensor_scalar(raw[:, par, :, c, :], raw[:, par, :, c, :],
                                    cst[:, bass.ds(g * GRP + c, 1), 0], cst[:, bass.ds(g * GRP + c, 1), 1],
                                    ALU.subtract, ALU.mult).then_inc(norm_done, 1)
                dve.wait_ge(norm_done, g * (GRP + EDGES - 1) + GRP)
                flat = raw[:, par].rearrange("p i c j -> p (i c) j")
                edges = [(flat[:, :, 0], 0), (flat[:, :, TJ - 1], 1),
                         (raw[:, par, 0].rearrange("p c j -> p (c j)"), 2), (raw[:, par, TI - 1].rearrange("p c j -> p (c j)"), 3)]
                for n, (e, m) in enumerate(edges):
                    ins = V.tensor_scalar(e, e, side[:, m:m + 1], None, ALU.mult)
                    if n < EDGES - 1:
                        ins.then_inc(norm_done, 1)
                        dve.wait_ge(norm_done, g * (GRP + EDGES - 1) + GRP + n + 1)
                    else:
                        ins.then_inc(edge_done, 1)

            def low(g, par):
                dve.wait_ge(hi_done, g + 1)
                dve.wait_ge(edge_done, g + 1)
                if not (isinstance(g, int) and g < 2):
                    dve.wait_ge(conv_done, g * GRP - GRP)
                V.tensor_tensor(lo[:, par].rearrange("p i c j -> p (i c j)"), raw[:, par].rearrange("p i c j -> p (i c j)"),
                                hi[:, par].rearrange("p i c j -> p (i c j)"), ALU.subtract).then_inc(lo_done, 1)

            def bring(g, n):
                dve.wait_ge(back_done, g * FILLS + n + 1)
                bd, q = n // (FILLS // NBAND), n % (FILLS // NBAND)
                if n % (FILLS // NBAND) == 0 and not (at(g, 0)):
                    dve.wait_ge(out_done[bd], g * 16)
                src = bbank[n % NBB][:, :].rearrange("p (t y x) -> p t y x", t=TPB, y=TH)[:, :, ::-1, ::-1]
                dst = rows[:, bd, :, q * TPB * TW:(q + 1) * TPB * TW].rearrange("p y (t x) -> p t y x", t=TPB)
                V.tensor_copy(dst, src).then_inc(rows_done, 1)

            normalise(0, 0)
            low(0, 0)

            def step(g, par, inner=False):
                back = inner or g >= 1
                more = inner or g + 1 < NG
                if more:
                    normalise(g + 1, 1 - par)
                for n in range(FILLS):
                    if back:
                        bring(g - 1, n)
                    if n == 3 and more:
                        low(g + 1, 1 - par)

            run(dve, step, tail=NG - 2)

        @block.tensor
        def _(pe):
            FIRST_BACK = 2

            def back(g, par, n):
                if not (at(g, 0) and n < NBB):
                    pe.wait_ge(rows_done, g * FILLS + n - NBB + 1)
                bd, q = n // (FILLS // NBAND), n % (FILLS // NBAND)
                for k in range(TPB):
                    ins = nc.tensor.transpose(bbank[n % NBB][:, k * P:(k + 1) * P],
                                              res[:, par, bd, q * TPB + k].rearrange("p c i -> p (c i)"), ident[:, :])
                ins.then_inc(back_done, 1)

            def step(g, par, inner=False):
                live = inner or g < NG
                if live:
                    pe.wait_ge(lo_done, g + 1)
                for c in range(GRP):
                    if live:
                        rnd = c // NTOEP
                        pe.wait_ge(toep_in[c % NTOEP], g * (16 * GRP // NTOEP) + 16 * (rnd + 1))
                        if inner or g >= 1 or c >= NCB:
                            pe.wait_ge(res_done, g * GRP + c - NCB + 1)
                        n = 0
                        for s, u in shift:
                            rows_in = min(OI, TI - s)
                            out = cbank[c % NCB][:, 0:rows_in * OJ].rearrange("p (i j) -> p i j", j=OJ)
                            for part, x in ((0, hi), (0, lo), (1, hi)):
                                ins = nc.tensor.matmul(
                                    out, toep[:, c % NTOEP, :].rearrange("p (s m v) -> p s v m", s=NS, m=P)[:, s, u * 2 + part],
                                    x[:, par, s:s + rows_in, c, u:u + OJ],
                                    start=n == 0, stop=n == 3 * len(shift) - 1, skip_group_check=True)
                                n += 1
                        ins.then_inc(conv_done, 1)
                    f = c - FIRST_BACK
                    if (inner or g >= 1) and 0 <= f < FILLS:
                        if f == 0:
                            pe.wait_ge(res_done, g * GRP)
                        back(g - 1, 1 - par, f)

            run(pe, step)


def mk_conv_kernel(nc, a, out):
    x3 = a["x"].rearrange("a c h w -> (a c) (h w)")
    out3 = out.rearrange("a c h w -> (a c) (h w)")
    rq_dram = nc.dram_tensor("norm_scratch", [2 * C], F32).ap()
    v_dram = nc.dram_tensor("v_scratch", [C, VROWS * PW], F32).ap()
    pt_dram = nc.dram_tensor("attention_scratch", [C, C], F32).ap()
    patch_dram = nc.dram_tensor("patch_scratch", [P, NG, TI, GRP * TJ], F32).ap()
    toep_dram = nc.dram_tensor("toeplitz_scratch", [C, TW, 2 * NU * JR * TW], F16).ap()
    const_dram = nc.dram_tensor("constant_scratch", [C, 3], F32).ap()
    with ExitStack() as ctx:
        def sb(name, shape):
            return ctx.enter_context(nc.sbuf_tensor(name, shape, F32))

        ident = sb("ident", [P, P])
        member = sb("member", [P, CB, C])
        mean, rstd = sb("mean", [P, CB]), sb("rstd", [P, CB])
        kern = sb("kern", [P, CB, KL, KL])
        scale, shift = sb("scale", [P, 3, CB]), sb("shift", [P, 3, CB])
        REC0, REC1 = STEPS * (CHUNK // 512), STEPS * 3 + 1
        norms = [a[f"{n}_{k}"] for k in "lsi" for n in "gbmv"]
        with ExitStack() as gram_bank:
            gram = gram_bank.enter_context(nc.psum_tensor("gram", [P, 512], F32))
            with (nc.sbuf_tensor("whi", [P, CB, 3 * C], F16) as whi, nc.sbuf_tensor("wlo", [P, CB, 3 * C], F16) as wlo):
                with nc.sbuf_tensor("stats0", [P, CB, REC0, 6], F32) as stats:
                    stage_statistics(nc, x3, stats, a["w_qkv_T"], whi, wlo, a["w_large"], a["w_small"], norms,
                                     kern, scale, shift, ident, member)
                    group_affine(nc, "g0", stats, member, mean, rstd)
                stage_qkv(nc, x3, whi, wlo, a["b_qkv"], a["w_dw"], a["b_dw"], mean, rstd, ident, kern, rq_dram, v_dram,
                          toep_dram, gram)
            stats = sb("stats1", [P, CB, REC1, 6])
            with ExitStack() as inner:
                pt = inner.enter_context(nc.sbuf_tensor("pt", [P, CB, C], F32))
                project = project_start(nc, inner, x3, v_dram, a["w_proj_T"], a["b_proj"])
                stage_attention(nc, gram, rq_dram, a["temperature"], [a["a1"], a["a2"], a["a3"], a["a4"]],
                                pt_dram, ident, pt, project)
                gram_bank.close()
                stage_project(nc, project, pt, ident, stats, patch_dram)
        conv = depthwise_start(nc, ctx, patch_dram)
        group_affine(nc, "g1", stats, member, mean, rstd, conv)
        stage_kernels(nc, kern, scale, shift, mean, rstd, toep_dram, const_dram)
        stage_depthwise(nc, conv, toep_dram, const_dram, ident, out3)


def kernel(**inputs):
    import numpy as np
    import concourse.bacc as bacc
    from concourse import mybir as mb
    from concourse.bass_utils import run_bass_kernel_spmd

    nc = bacc.Bacc("TRN2", target_bir_lowering=False, num_devices=1)
    arrays, handles = {}, {}
    for name, value in inputs.items():
        short = name.split("conv_")[-1]
        value = np.asarray(value)
        if short in ("w_qkv", "w_proj"):
            short, value = short + "_T", value.T
        value = np.ascontiguousarray(value)
        arrays[f"in_{short}"] = value
        handles[short] = nc.dram_tensor(f"in_{short}", value.shape, mb.dt.from_np(value.dtype), kind="ExternalInput").ap()
    out = nc.dram_tensor("out_0", (1, C, H, W), F32, kind="ExternalOutput").ap()
    mk_conv_kernel(nc, handles, out)
    result = run_bass_kernel_spmd(nc, [arrays], core_ids=[0])
    return result.results[0]["out_0"]
```
